# Optimizing a Trainium2 kernel written in Bass

```python
import numpy as np
import jax
import jax.numpy as jnp

def _softmax(x, axis=-1):
    return jax.nn.softmax(x, axis=axis)

def _gelu(x):
    return jax.nn.gelu(x, approximate=True)

def _silu(x):
    return jax.nn.silu(x)

def _sigmoid(x):
    return jax.nn.sigmoid(x)

def _layernorm(x, axis=-1, eps=1e-05):
    m = jnp.mean(x, axis=axis, keepdims=True)
    v = jnp.var(x, axis=axis, keepdims=True)
    return (x - m) / jnp.sqrt(v + eps)

def _scatter_add(tgt, idx, src, axis=0):
    return tgt.at[idx].add(src)

def _segment_sum(src, seg, n):
    return jax.ops.segment_sum(src, seg, n)
kernel_name = 'mk_flamingo_gated_d1_seqx_r8_d92ec9'

def setup_inputs(seed: int=0):
    np.random.seed(seed)
    _w = jnp.asarray

    def _rec_inputs():
        import jax
        import jax.numpy as jnp
        _rk = jax.random.key(seed)
        x = -0.0003929 + 0.9999 * jax.random.normal(jax.random.fold_in(_rk, 1), (4, 256, 512), jnp.float32)
        _lenS = 256 - jax.random.randint(jax.random.fold_in(_rk, 7), (4,), 0, max(1, 256 // 4) + 1, jnp.int32)
        _lenS2 = 1601 - jax.random.randint(jax.random.fold_in(_rk, 8), (4,), 0, max(1, 1601 // 4) + 1, jnp.int32)
        _ctx_4096P = jax.random.normal(jax.random.fold_in(_rk, 11), (4, 16, 512), jnp.float32)
        _ctx_4096c = jax.random.dirichlet(jax.random.fold_in(_rk, 511), 0.3 * jnp.ones((16,), jnp.float32), (4, 1601))
        _ctx_4096t = jnp.einsum('bsk,bkd->bsd', _ctx_4096c, _ctx_4096P)
        _ctx_4096t = _ctx_4096t * jax.lax.rsqrt(jnp.mean(jnp.square(_ctx_4096t)) + 1e-12) * 0.953939
        ctx_4096 = 2.81802e-05 + 1.00001 * (_ctx_4096t + 0.3 * jax.random.normal(jax.random.fold_in(_rk, 611), (4, 1601, 512), jnp.float32))
        _g = jax.random.normal(jax.random.fold_in(_rk, 9001), (2, 1), jnp.float32)
        _g = jnp.sign(_g) * jnp.maximum(jnp.abs(_g), 1.0) + (_g == 0) * 1.0
        g_xattn = _g[0]
        g_ffn = _g[1]
        return (x, ctx_4096, g_xattn, g_ffn)
    x, ctx_4096, g_xattn, g_ffn = _rec_inputs()

    def _L0_xattn_setup():
        import jax, jax.numpy as jnp
        import numpy as np
        HID = 512
        NHEAD = 32
        NKV = 8
        HDIM = 128
        G = NHEAD // NKV
        key = jax.random.key(seed)
        ks = jax.random.split(key, 6)
        s = 0.02
        B, L = (2, 256)
        return {'query': jax.random.normal(ks[0], (B, L, HID), jnp.float32), 'kv': jax.random.normal(ks[1], (B, L, HID), jnp.float32), 'Wq': jax.random.normal(ks[2], (HID, NHEAD * HDIM), jnp.float32) * s, 'bq': jnp.zeros((NHEAD * HDIM,), jnp.float32), 'Wkv': jax.random.normal(ks[3], (HID, 2 * NKV * HDIM), jnp.float32) * s, 'bkv': jnp.zeros((2 * NKV * HDIM,), jnp.float32), 'Wo': jax.random.normal(ks[4], (NHEAD * HDIM, HID), jnp.float32) * s, 'bo': jnp.zeros((HID,), jnp.float32)}
    _L0_xattn_all = _L0_xattn_setup()
    _L0_xattn_in = {k: v for k, v in _L0_xattn_all.items() if k in ('Wq', 'bq', 'Wkv', 'bkv', 'Wo', 'bo')}
    del _L0_xattn_all

    def _L0_ffn_setup():
        import jax, jax.numpy as jnp
        import numpy as np
        D_IN = 512
        D_OUT = 512
        RANK = 16
        NUM_EXPERTS = 8
        TOP_K = 2
        SCALING = 32.0 / RANK
        key = jax.random.key(seed)
        ks = jax.random.split(key, 6)
        x = jax.random.normal(ks[0], (4, 256, D_IN), dtype=jnp.float32)
        W_base = jax.random.normal(ks[1], (D_OUT, D_IN), dtype=jnp.float32) * (1.0 / np.sqrt(D_IN))
        b_base = jax.random.normal(ks[2], (D_OUT,), dtype=jnp.float32) * 0.01
        W_router = jax.random.normal(ks[3], (NUM_EXPERTS, D_IN), dtype=jnp.float32) * 0.01
        A_stack = jax.random.uniform(ks[4], (NUM_EXPERTS, RANK, D_IN), dtype=jnp.float32, minval=-1.0, maxval=1.0) * (1.0 / np.sqrt(D_IN))
        B_stack = jax.random.normal(ks[5], (NUM_EXPERTS, D_OUT, RANK), dtype=jnp.float32) * 0.02
        return {'x': x, 'W_base': W_base, 'b_base': b_base, 'W_router': W_router, 'A_stack': A_stack, 'B_stack': B_stack}
    _L0_ffn_all = _L0_ffn_setup()
    _L0_ffn_in = {k: v for k, v in _L0_ffn_all.items() if k in ('W_base', 'b_base', 'W_router', 'A_stack', 'B_stack')}
    del _L0_ffn_all
    return {'x': x, 'ctx_4096': ctx_4096, 'g_xattn': g_xattn, 'g_ffn': g_ffn, 'L0_xattn_Wq': _L0_xattn_in['Wq'], 'L0_xattn_bq': _L0_xattn_in['bq'], 'L0_xattn_Wkv': _L0_xattn_in['Wkv'], 'L0_xattn_bkv': _L0_xattn_in['bkv'], 'L0_xattn_Wo': _L0_xattn_in['Wo'], 'L0_xattn_bo': _L0_xattn_in['bo'], 'L0_ffn_W_base': _L0_ffn_in['W_base'], 'L0_ffn_b_base': _L0_ffn_in['b_base'], 'L0_ffn_W_router': _L0_ffn_in['W_router'], 'L0_ffn_A_stack': _L0_ffn_in['A_stack'], 'L0_ffn_B_stack': _L0_ffn_in['B_stack']}

def reference(x, ctx_4096, g_xattn, g_ffn, L0_xattn_Wq, L0_xattn_bq, L0_xattn_Wkv, L0_xattn_bkv, L0_xattn_Wo, L0_xattn_bo, L0_ffn_W_base, L0_ffn_b_base, L0_ffn_W_router, L0_ffn_A_stack, L0_ffn_B_stack):
    import jax
    import jax.numpy as jnp

    def _L0_xattn_ref(query, kv, Wq, bq, Wkv, bkv, Wo, bo):
        import jax, jax.numpy as jnp
        import numpy as np
        HID = 512
        NHEAD = 32
        NKV = 8
        HDIM = 128
        G = NHEAD // NKV
        B, L, _ = query.shape
        Lk = kv.shape[1]
        scale = jnp.asarray(1.0 / np.sqrt(HDIM), query.dtype)
        q = (query @ Wq + bq).reshape(B, L, NKV, G, HDIM)
        k_, v_ = jnp.split(kv @ Wkv + bkv, 2, axis=-1)
        k = k_.reshape(B, Lk, NKV, HDIM)
        v = v_.reshape(B, Lk, NKV, HDIM)
        scores = jnp.einsum('blkgd,bmkd->bkglm', q, k) * scale
        attn = jax.nn.softmax(scores, axis=-1)
        o = jnp.einsum('bkglm,bmkd->blkgd', attn, v).reshape(B, L, NHEAD * HDIM)
        return o @ Wo + bo

    def _L0_ffn_ref(x, W_base, b_base, W_router, A_stack, B_stack):
        import jax, jax.numpy as jnp
        import numpy as np
        D_IN = 512
        D_OUT = 512
        RANK = 16
        NUM_EXPERTS = 8
        TOP_K = 2
        SCALING = 32.0 / RANK
        orig_shape = x.shape
        xf = x.reshape(-1, D_IN)
        logits = xf @ W_router.T
        probs = jax.nn.softmax(logits, axis=-1)
        topk_p, topk_i = jax.lax.top_k(probs, TOP_K)
        topk_p = topk_p / jnp.sum(topk_p, axis=-1, keepdims=True)
        combine = jnp.sum(jax.nn.one_hot(topk_i, NUM_EXPERTS, dtype=xf.dtype) * topk_p[..., None], axis=1)
        h = jnp.einsum('nd,erd->ner', xf, A_stack)
        h = h * combine[..., None]
        lora_out = jnp.einsum('ner,eor->no', h, B_stack) * SCALING
        base_out = xf @ W_base.T + b_base
        out = base_out + lora_out
        return out.reshape(orig_shape[:-1] + (D_OUT,))
    x = x + jnp.tanh(g_xattn[0]) * _L0_xattn_ref(_layernorm(x, axis=-1), ctx_4096, L0_xattn_Wq, L0_xattn_bq, L0_xattn_Wkv, L0_xattn_bkv, L0_xattn_Wo, L0_xattn_bo)
    x = x + jnp.tanh(g_ffn[0]) * _L0_ffn_ref(_layernorm(x, axis=-1), L0_ffn_W_base, L0_ffn_b_base, L0_ffn_W_router, L0_ffn_A_stack, L0_ffn_B_stack)
    return x

_drawn_inputs = setup_inputs


def setup_inputs(seed=0):
    import zlib

    import numpy as np

    out = dict(_drawn_inputs(seed))
    spreads = {'L0_xattn_bq': (0.0, 2.0), 'L0_xattn_bkv': (0.0, 0.1), 'L0_xattn_bo': (0.0, 0.1)}
    factors = {'L0_xattn_Wq': 3.912, 'L0_ffn_b_base': 8.0}
    for name, (base, spread) in spreads.items():
        noise = np.random.default_rng([zlib.crc32(name.encode()), seed]).standard_normal(out[name].shape)
        drawn = base * np.exp(spread * noise) if base else spread * noise
        out[name] = jnp.asarray(drawn.astype(out[name].dtype))
    for name, factor in factors.items():
        out[name] = (out[name] * factor).astype(out[name].dtype)
    return out
```

```python
import concourse.bass as bass
from concourse import mybir
from contextlib import ExitStack

F32 = mybir.dt.float32
F32R = mybir.dt.float32r
U32 = mybir.dt.uint32
ALU = mybir.AluOpType
ACT = mybir.ActivationFunctionType
AX = mybir.AxisListType

BATCH, TOK, DM = 4, 256, 512
HEADS, KVH, HD = 32, 8, 128
GQ = HEADS // KVH
KEYS = 1601
P = 128
SCALE = float(HD) ** -0.5
EPS = 1e-5
EXPERTS, RANK = 8, 16
LORA_SCALE = 32.0 / RANK

NT = BATCH * TOK // P
DC = DM // P
KT = -(-KEYS // P)
TAIL = KEYS - (KT - 1) * P
KEYS_E = KEYS + KEYS % 2
CW = 402
CHUNKS = [(c * CW, min(CW, KEYS_E - c * CW), min(CW, KEYS - c * CW)) for c in range(4)]
BANK = 512
DMA_SCRATCH = 16640
NSTEP = KVH * BATCH * 2
PG = 8


def keys_in(kt):
    return P if kt < KT - 1 else TAIL


def step_units():
    count = dict(O=0, T=0, P=0, S=0)
    units = []
    for kind in "OOSTTSSSTPTPTPPTTSSSTSPPPTPTSSPTSTPSTPTPPSSSS":
        i = count[kind]
        count[kind] += 1
        units.append(("S", i // 4, i % 4) if kind == "S" else (kind, i))
    return units


def act_units():
    units = []
    count = dict(T=0, E=0, F=0)
    for kind in "TTTTTETFTTETFTTTTETFNEF":
        units.append((kind, count.get(kind, 0)))
        if kind in count:
            count[kind] += 1
    return units


def dve_units():
    units = []
    count = dict(A=0, T=0, M=0)
    for kind in "AAITMTMTMTMTTMTMMMTTTMMTTMMTNMLMMM":
        units.append((kind, count.get(kind, 0)))
        if kind in count:
            count[kind] += 1
    return units


def build(nc, x, ctxt, g_xattn, g_ffn, Wq, bq, Wkv, bkv, Wo, bo, W_base, b_base, W_router,
          A_stack, B_stack, out):
    es = ExitStack()
    q_dram = nc.dram_tensor("q_scratch", (HEADS, P, BATCH * TOK), F32, kind="Internal").ap()
    k_dram = nc.dram_tensor("k_scratch", (BATCH * KVH, P, KEYS), F32, kind="Internal").ap()
    v_dram = nc.dram_tensor("v_scratch", (BATCH * KVH, P, KT * HD), F32, kind="Internal").ap()

    top = [DMA_SCRATCH]

    def sb(name, shape, dt=F32, at=None):
        size = 4
        for s in shape[1:]:
            size *= s
        at = top[0] if at is None else at
        at = -(-at // 32) * 32
        top[0] = at + size
        return nc.alloc_sbuf_tensor_at(name, list(shape), dt, offset=at)

    def sem(name):
        return es.enter_context(nc.semaphore(name))

    ident = sb("ident", [P, P])
    bias_rows = sb("bias_rows", [HEADS + KVH, P])
    bqT = sb("bqT", [P, HEADS])
    bkT = sb("bkT", [P, KVH])
    half_neg = sb("half_neg", [P, NT])
    stats = sb("stats", [P, NT, 6])
    mv = sb("mv", [P, NT, 2])
    veps = sb("veps", [P, NT])
    rstd = sb("rstd", [P, NT])
    WbT = sb("WbT", [P, DC, DM])
    RAT = sb("RAT", [P, DC, EXPERTS + EXPERTS * RANK])
    BT = sb("BT", [EXPERTS * RANK, DM])
    base = top[0]

    wk = [sb("wk_hi", [P, DC, KVH * HD], F32R), sb("wk_lo", [P, DC, KVH * HD], F32R)]
    z_wv = top[0]
    wv = [sb("wv_hi", [P, DC, KVH * HD], F32R), sb("wv_lo", [P, DC, KVH * HD], F32R)]
    z_ctx = top[0]
    ctxT = [sb("ctxT_hi", [P, DC, KEYS_E], F32R), sb("ctxT_lo", [P, DC, KEYS_E], F32R)]
    z_raw = top[0]
    ctx_raw = sb("ctx_raw", [P, KT, DM])
    z_stage = top[0]
    k_stage = [sb(f"k_stage{i}", [P, KEYS]) for i in range(2)]
    v_stage = [sb(f"v_stage{i}", [P, KVH * HD]) for i in range(2)]
    bv_bc = sb("bv_bc", [P, KVH * HD])
    z_end = top[0]

    xT = [sb("xT_hi", [P, DC, BATCH * TOK], F32R, at=z_ctx), sb("xT_lo", [P, DC, BATCH * TOK], F32R)]
    wq_raw = [sb(f"wq_raw{i}", [P, DC, HD]) for i in range(GQ)]
    q_stage = [sb(f"q_stage{i}", [P, BATCH * TOK]) for i in range(2)]
    assert top[0] <= z_raw
    wq = [[sb(f"wq_hi{i}", [P, DC, HD], F32R, at=z_stage if i == 0 else None),
           sb(f"wq_lo{i}", [P, DC, HD], F32R)] for i in range(GQ)]
    assert top[0] <= z_end - 4 * KVH * HD
    xn = sb("xn", [P, NT, DM], at=z_end)
    wkv_raw = [sb(f"wkv_raw{i}", [P, 2 * KVH * HD]) for i in range(1)]
    ffn_raw = sb("ffn_raw", [P, DC, DM], at=z_raw)
    A_raw = sb("A_raw", [P, DM])
    R_raw = sb("R_raw", [EXPERTS, DM])
    B_raw = sb("B_raw", [P, DC, EXPERTS * RANK])

    kh = [[sb(f"k_hi{i}", [P, KEYS_E], F32R, at=base if i == 0 else None),
           sb(f"k_lo{i}", [P, KEYS_E], F32R)] for i in range(2)]
    q_raw = [sb(f"q_raw{i}", [P, 2, TOK]) for i in range(2)]
    assert top[0] <= z_wv
    v1 = [sb("v_hi1", [P, KT, HD], F32R), sb("v_lo1", [P, KT, HD], F32R)]
    pT = [[sb(f"pT_hi{i}", [P, BANK], F32R), sb(f"pT_lo{i}", [P, BANK], F32R)] for i in range(3)]
    r_bc = sb("r_bc", [P, BANK])
    o_f = sb("o_f", [P, BANK])
    oT = [sb("oT_hi", [P, BANK], F32R), sb("oT_lo", [P, BANK], F32R)]
    rows = sb("row_sums", [P, 2, 4, 2])
    rsum = sb("rsum", [P, 4])
    rinv = sb("rinv", [P, 4])
    mx = sb("mx", [P, 2, 3])
    nmax = sb("nmax", [P, 2, 1])
    assert top[0] <= z_ctx
    prob = [[sb(f"prob{i}_{t}", [P, KEYS], at=z_ctx if i + t == 0 else None) for t in range(4)]
            for i in range(2)]
    k_raw = sb("k_raw", [P, KEYS], at=max(top[0], z_raw))
    v_raw = sb("v_raw", [P, KT, HD])
    v0 = [sb("v_hi0", [P, KT, HD], F32R), sb("v_lo0", [P, KT, HD], F32R)]
    vh = [v0, v1]
    wo = [sb("wo_hi", [P, GQ, DM], F32R, at=max(top[0], z_stage)), sb("wo_lo", [P, GQ, DM], F32R)]
    wo_raw = sb("wo_raw", [P, GQ, DM])
    qh = [[sb(f"q_hi{i}", [P, 2 * TOK], F32R, at=max(top[0], z_end) if i == 0 else None),
           sb(f"q_lo{i}", [P, 2 * TOK], F32R)] for i in range(2)]
    acc = sb("acc", [P, NT, DM])

    bo_bc = sb("bo_bc", [P, DM], at=z_ctx)
    bb_bc = sb("bb_bc", [P, DM])
    gates = sb("gates", [P, 2])
    tg = sb("tanh_gates", [P, 2])
    iota_e = sb("iota_e", [P, EXPERTS])
    xr = sb("x_res", [P, NT, DM])
    f_y = [sb(f"f_y{i}", [P, DM]) for i in range(2)]
    f_x1 = [sb(f"f_x1_{i}", [P, DM]) for i in range(4)]
    z_f = top[0]
    f_xn = [sb(f"f_xn{i}", [P, DM], at=z_f if i == 0 else None) for i in range(2)]
    f_xT = [sb(f"f_xT{i}", [P, DC, P]) for i in range(2)]
    f_o = [sb(f"f_o{i}", [P, DM]) for i in range(2)]
    f_hc = [sb(f"f_hc{i}", [P, P]) for i in range(2)]
    f_hT = [sb(f"f_hT{i}", [P, P]) for i in range(2)]
    f_sm = [sb(f"f_small{i}", [P, 96]) for i in range(2)]
    f_ix = [sb(f"f_index{i}", [P, 8], U32) for i in range(2)]
    assert top[0] <= z_stage

    psum = es.enter_context(nc.psum_tensor("psum", [P, 8 * BANK], F32))

    def bank(i, w=BANK):
        return psum[:, i * BANK:i * BANK + w]

    x_ld = [sem(f"x_loaded{i}") for i in range(2)]
    wq_ld = [sem(f"wq_loaded{i}") for i in range(GQ)]
    wkv_ld = sem("wkv_loaded")
    bias_ld = sem("bias_loaded")
    bv_ld = sem("bv_loaded")
    ffn_ld = sem("ffn_weights_loaded")
    ctx_ld = sem("ctx_loaded")
    ctx_tail_ld = sem("ctx_tail_loaded")
    id_rdy = sem("ident_ready")
    cst = sem("constants_ready")
    x_stat = sem("x_stats")
    x_var = sem("x_var_ready")
    x_rstd = sem("x_rstd_ready")
    xn_rdy = sem("xn_ready")
    xT_mm = sem("xT_transposed")
    xT_hi_s = sem("xT_hi_ready")
    xT_lo_s = sem("xT_lo_ready")
    b_mm = sem("bias_transposed")
    b_rdy = sem("bias_ready")
    wq_hi_s = sem("wq_hi_ready")
    wq_split = sem("wq_split")
    q_mm = sem("q_multiplied")
    q_ev = sem("q_evacuated")
    q_st = [sem(f"q_stored{i}") for i in range(2)]
    wkv_hi_s = sem("wkv_hi_ready")
    wkv_split = sem("wkv_split")
    f_mm = sem("ffn_weights_transposed")
    f_ev = sem("ffn_weights_evacuated")
    c_t = sem("ctx_transposed")
    c_hi = sem("ctxT_hi_ready")
    c_lo = sem("ctxT_lo_ready")
    k_mm = sem("k_multiplied")
    k_ev = sem("k_evacuated")
    k_st = [sem(f"k_stored{i}") for i in range(2)]
    v_mm = sem("v_multiplied")
    v_ev = sem("v_evacuated")
    v_st = [sem(f"v_stored{i}") for i in range(2)]
    pad = sem("pad_cleared")
    acc_0 = sem("acc_cleared")
    split_go = sem("split_may_start")
    k_ld = sem("k_loaded")
    v_ld = sem("v_loaded")
    vt_ld = sem("v_tail_loaded")
    q_ld = [sem(f"q_loaded{i}") for i in range(2)]
    wo_ld = sem("wo_loaded")
    k_hi_s = sem("k_hi_ready")
    k_split = sem("k_split")
    v_hi_s = sem("v_hi_ready")
    v_split = sem("v_split")
    q_hi_s = sem("q_hi_ready")
    q_split = sem("q_split")
    wo_hi_s = sem("wo_hi_ready")
    wo_split = sem("wo_split")
    s_mm = sem("scores_multiplied")
    mx_s = sem("chunk_max_ready")
    nm_s = sem("neg_max_ready")
    ex_a = sem("exp_first_chunks")
    ex_b = sem("exp_last_chunk")
    t_mm = sem("prob_transposed")
    pt_hi = sem("pT_hi_ready")
    pt_lo = sem("pT_lo_ready")
    rs_s = sem("row_sum_ready")
    ri_s = sem("row_inverse_ready")
    r_cp = sem("row_inverse_broadcast")
    pv_mm = sem("pv_multiplied")
    o_nrm = sem("o_normalised")
    o_hi_s = sem("o_hi_ready")
    o_split = sem("o_split")
    o_mm = sem("o_projected")
    o_add = sem("o_accumulated")
    fx_ld = sem("ffn_inputs_loaded")
    g_rdy = sem("gates_ready")
    fv = sem("ffn_vector_steps")
    f_var = sem("ffn_var_ready")
    f_rstd = sem("ffn_rstd_ready")
    f_xn_s = sem("ffn_xn_ready")
    f_tr = sem("ffn_xT_transposed")
    f_xT_s = sem("ffn_xT_ready")
    f_ra = sem("ffn_router_and_a_ready")
    f_nm = sem("ffn_router_neg_max")
    f_ex = sem("ffn_router_exp")
    f_hc_s = sem("ffn_expert_hidden_ready")
    f_ht = sem("ffn_hidden_transposed")
    f_hT_s = sem("ffn_hT_ready")
    f_out = sem("ffn_product_ready")
    f_fin = sem("ffn_tile_ready")
    f_st = [sem(f"out_stored{i}") for i in range(2)]

    def need(eng, s, value):
        if isinstance(value, int) and value <= 0:
            return
        eng.wait_ge(s, value)

    def product(o, a, b, first, last):
        nc.tensor.matmul(o, a[1], b[0], start=first, stop=False)
        nc.tensor.matmul(o, a[0], b[1], start=False, stop=False)
        return nc.tensor.matmul(o, a[0], b[0], start=False, stop=last)

    def f32(ap):
        return ap.bitcast(F32)

    WQ_V = Wq.rearrange("(k p) n -> p k n", p=P)
    WKV_V = Wkv.rearrange("(k p) n -> k p n", p=P)
    X_V = x.rearrange("b (t p) n -> p (b t) n", p=P)
    OUT_V = out.rearrange("b (t p) n -> (b t) p n", p=P)
    VB = v_dram.rearrange("(b g) p (t d) -> b p t g d", b=BATCH, d=HD)
    Q_B = q_dram.rearrange("h d (b t) -> h d b t", b=BATCH)
    PE_UNITS, ACT_UNITS, DVE_UNITS = step_units(), act_units(), dve_units()
    FFN_GROUPS = DC * DC + 3 * DC

    def ffn_piece(n):
        if n < DC * DC:
            c, k = n // DC, n % DC
            return (ffn_raw[:, c, k * P:(k + 1) * P], P, P), WbT[:, k, c * P:(c + 1) * P]
        n -= DC * DC
        if n < DC:
            return (A_raw[:, n * P:(n + 1) * P], P, P), RAT[:, n, EXPERTS:EXPERTS + P]
        n -= DC
        if n < DC:
            return (R_raw[:, n * P:(n + 1) * P], P, EXPERTS), RAT[:, n, 0:EXPERTS]
        n -= DC
        return (B_raw[:, n, :], P, P), BT[:, n * P:(n + 1) * P]

    block = es.enter_context(nc.Block())

    @block.sync
    def _(sp):
        for i in range(2):
            sp.dma_start(xn[:, 4 * i:4 * i + 4, :], X_V[:, 4 * i:4 * i + 4, :]).then_inc(x_ld[i], 16)

        def load_wq(g, hh):
            sp.dma_start(wq_raw[hh][:, :, :], WQ_V[:, :, bass.ds(g * GQ * HD + hh * HD, HD)])\
              .then_inc(wq_ld[hh], 16)

        for hh in range(GQ):
            load_wq(0, hh)

        def q_round(g, last):
            for hh in range(GQ):
                if not last:
                    sp.wait_ge(wq_split, GQ * g + hh + 1)
                    load_wq(g + 1, hh)
                sp.wait_ge(q_ev, 2 * (GQ * g + hh) + 2)
                sp.dma_start(q_dram[bass.ds(GQ * g + hh, 1), :, :].rearrange("a p n -> (a p) n"),
                             q_stage[hh % 2][:, :]).then_inc(q_st[hh % 2], 16)

        with sp.Fori(0, KVH - 1) as g:
            q_round(g, False)
        q_round(KVH - 1, True)

        def load_ctx(b):
            sp.dma_start(ctx_raw[:, 0:KT - 1, :],
                         ctxt[bass.ds(b, 1), 0:(KT - 1) * P, :].rearrange("a (t p) n -> p (a t) n", p=P))\
              .then_inc(ctx_ld, 16)
            sp.dma_start(ctx_raw[0:TAIL, KT - 1, :],
                         ctxt[bass.ds(b, 1), (KT - 1) * P:KEYS, :].rearrange("a p n -> (a p) n"))\
              .then_inc(ctx_tail_ld, 16)

        sp.wait_ge(f_mm, FFN_GROUPS)
        load_ctx(0)

        def store_v(b, kt):
            n = keys_in(kt)
            sp.wait_ge(v_ev, 2 * (KT * b + kt + 1))
            sp.dma_start(VB[bass.ds(b, 1), 0:n, kt, :, :].rearrange("a p g d -> p (a g) d"),
                         v_stage[kt % 2][0:n, :].rearrange("p (g d) -> p g d", d=HD))\
              .then_inc(v_st[kt % 2], 16)

        def kv_round(b, first, last):
            if not first:
                for kt in range(KT):
                    store_v(b - 1, kt)
            if not last:
                sp.wait_ge(c_t, KT * (b + 1))
                load_ctx(b + 1)
            for h in range(KVH):
                sp.wait_ge(k_ev, 4 * (KVH * b + h + 1))
                sp.dma_start(k_dram[bass.ds(b * KVH + h, 1), :, :].rearrange("a p n -> (a p) n"),
                             k_stage[h % 2][:, :]).then_inc(k_st[h % 2], 16)

        kv_round(0, True, False)
        with sp.Fori(1, BATCH - 1) as b:
            kv_round(b, False, False)
        kv_round(BATCH - 1, False, True)
        for i in range(2):
            sp.wait_ge(q_st[i], 16 * HEADS // 2)
            sp.wait_ge(k_st[i], 16 * BATCH * KVH // 2)

        def load_k(i, g, b):
            need(sp, k_split, i)
            sp.dma_start(k_raw[:, :], k_dram[bass.ds(b * KVH + g, 1), :, :].rearrange("a p n -> (a p) n"))\
              .then_inc(k_ld, 16)

        def load_v(i, g, b):
            need(sp, v_split, i)
            src = v_dram[bass.ds(b * KVH + g, 1), :, :].rearrange("a p n -> (a p) n")
            sp.dma_start(v_raw[:, 0:KT - 1, :], src[:, 0:(KT - 1) * HD].rearrange("p (t d) -> p t d", d=HD))\
              .then_inc(v_ld, 16)
            sp.dma_start(v_raw[0:TAIL, KT - 1, :], src[0:TAIL, (KT - 1) * HD:KT * HD]).then_inc(vt_ld, 16)

        def load_q(n, g, b, j):
            need(sp, q_split, n - 1)
            sp.dma_start(q_raw[j][:, :, :],
                         Q_B[bass.ds(GQ * g + 2 * j, 2), :, b, :].rearrange("h d t -> d h t"))\
              .then_inc(q_ld[j], 16)

        def load_wo(g):
            need(sp, wo_split, g)
            sp.dma_start(wo_raw[:, :, :], Wo[bass.ds(g * GQ * HD, GQ * HD), :]
                         .rearrange("(h d) n -> d h n", d=HD)).then_inc(wo_ld, 16)

        def a_loads(g, first):
            for b in range(BATCH):
                i = BATCH * g + b
                load_k(i, g, b)
                load_q(2 * i, g, b, 0)
                if b == 1:
                    load_wo(g)
                load_q(2 * i + 1, g, b, 1)
                if first and b == 0:
                    for kt in range(KT):
                        store_v(BATCH - 1, kt)
                    sp.wait_ge(v_st[0], 16 * BATCH * ((KT + 1) // 2))
                    sp.wait_ge(v_st[1], 16 * BATCH * (KT // 2))
                load_v(i, g, b)

        a_loads(0, True)
        with sp.Fori(1, KVH) as g:
            a_loads(g, False)

        sp.wait_ge(t_mm, (KT + 1) * NSTEP)
        sp.dma_start(xr[:, :, :], X_V).then_inc(fx_ld, 16)
        sp.dma_start(bo_bc[:, :], bo.partition_broadcast(P)).then_inc(fx_ld, 16)
        sp.dma_start(bb_bc[:, :], b_base.partition_broadcast(P)).then_inc(fx_ld, 16)
        sp.dma_start(gates[:, 0:1], g_xattn.partition_broadcast(P)).then_inc(fx_ld, 16)
        sp.dma_start(gates[:, 1:2], g_ffn.partition_broadcast(P)).then_inc(fx_ld, 16)
        for t in range(NT):
            sp.wait_ge(f_fin, t + 1)
            sp.dma_start(OUT_V[t], f_o[t % 2][:, :]).then_inc(f_st[t % 2], 16)
        for i in range(2):
            sp.wait_ge(f_st[i], 16 * NT // 2)

    @block.gpsimd
    def _(pool):
        pool.memset(ident[:, :], 0.0).then_inc(id_rdy, 1)
        pool.memset(half_neg[:, :], -0.5).then_inc(cst, 1)
        pool.wait_ge(id_rdy, 1)
        pool.affine_select(out=ident[:, :], in_=ident[:, :], compare_op=ALU.not_equal, fill=1.0,
                           base=0, pattern=[[-1, P]], channel_multiplier=1).then_inc(id_rdy, 1)
        pool.wait_ge(cst, 1)
        for i in range(2):
            pool.wait_ge(x_var, i + 1)
            sl = slice(4 * i, 4 * i + 4)
            pool.tensor_tensor(rstd[:, sl], veps[:, sl], half_neg[:, sl], ALU.pow).then_inc(x_rstd, 1)

        def split(raw, hi, lo, hi_s, n, split_s):
            pool.sem_inc(split_go, 1)
            pool.tensor_scalar(hi, raw, 1.0, 0.0, ALU.mult, ALU.add).then_inc(hi_s, 1)
            pool.wait_ge(hi_s, n + 1)
            pool.tensor_tensor(lo, raw, f32(hi), ALU.subtract).then_inc(split_s, 1)

        def q_round(g, first):
            for hh in range(GQ):
                h = GQ * g + hh
                pool.wait_ge(wq_ld[hh], 16 * (g + 1))
                if not first:
                    pool.wait_ge(q_mm, 2 * (h - GQ + 1))
                split(wq_raw[hh][:, :, :], wq[hh][0][:, :, :], wq[hh][1][:, :, :], wq_hi_s, h, wq_split)

        q_round(0, True)
        with pool.Fori(1, KVH) as g:
            q_round(g, False)

        pool.wait_ge(k_mm, 4 * BATCH * KVH)
        for i in range(2):
            for part in kh[i]:
                pool.memset(f32(part[:, KEYS:KEYS_E]), 0.0).then_inc(pad, 1)
        pool.memset(acc[:, :, :], 0.0).then_inc(acc_0, 1)

        def a_splits(g, first):
            for b in range(BATCH):
                i = BATCH * g + b
                pool.wait_ge(k_ld, 16 * (i + 1))
                if not first or i >= 2:
                    pool.wait_ge(s_mm, 24 * (i - 1))
                split(k_raw[:, :], kh[b % 2][0][:, 0:KEYS], kh[b % 2][1][:, 0:KEYS], k_hi_s, i, k_split)
                for j in range(2):
                    n = 2 * i + j
                    if b == 1 and j == 1:
                        pool.wait_ge(wo_ld, 16 * (g + 1))
                        if not first:
                            pool.wait_ge(o_mm, 2 * PG * g)
                        else:
                            pool.wait_ge(v_mm, 2 * KT * BATCH)
                        split(wo_raw[:, :, :], wo[0][:, :, :], wo[1][:, :, :], wo_hi_s, g, wo_split)
                    pool.wait_ge(q_ld[j], 16 * (i + 1))
                    if not first or n >= 2:
                        pool.wait_ge(s_mm, 12 * (n - 1))
                    split(q_raw[j][:, :, :].rearrange("p h t -> p (h t)"), qh[j][0][:, :],
                          qh[j][1][:, :], q_hi_s, n, q_split)
                pool.wait_ge(v_ld, 16 * (i + 1))
                pool.wait_ge(vt_ld, 16 * (i + 1))
                if first and b == 1:
                    pool.wait_ge(v_mm, 2 * KT * BATCH)
                if not first or i >= 2:
                    pool.wait_ge(pv_mm, KT * (2 * i - 2))
                hi, lo = vh[b % 2]
                full = slice(0, KT - 1)
                pool.sem_inc(split_go, 1)
                pool.tensor_scalar(hi[:, full, :], v_raw[:, full, :], 1.0, 0.0, ALU.mult, ALU.add)\
                    .then_inc(v_hi_s, 1)
                pool.tensor_scalar(hi[0:TAIL, KT - 1, :], v_raw[0:TAIL, KT - 1, :], 1.0, 0.0,
                                   ALU.mult, ALU.add).then_inc(v_hi_s, 1)
                pool.wait_ge(v_hi_s, 2 * i + 2)
                pool.tensor_tensor(lo[:, full, :], v_raw[:, full, :], f32(hi[:, full, :]), ALU.subtract)
                pool.tensor_tensor(lo[0:TAIL, KT - 1, :], v_raw[0:TAIL, KT - 1, :],
                                   f32(hi[0:TAIL, KT - 1, :]), ALU.subtract).then_inc(v_split, 1)

        a_splits(0, True)
        with pool.Fori(1, KVH) as g:
            a_splits(g, False)

        pool.wait_ge(t_mm, (KT + 1) * NSTEP)
        pool.iota(iota_e[:, :], [[1, EXPERTS]], base=0, channel_multiplier=0,
                  allow_small_or_imprecise_dtypes=True).then_inc(g_rdy, 1)
        for t in range(NT):
            pool.wait_ge(f_var, t + 1)
            pool.tensor_tensor(rstd[:, t:t + 1], veps[:, t:t + 1], half_neg[:, t:t + 1], ALU.pow)\
                .then_inc(f_rstd, 1)

    @block.scalar
    def _(act):
        act.dma_start(bias_rows[0:HEADS, :], bq.rearrange("(h d) -> h d", d=HD)).then_inc(bias_ld, 16)
        act.dma_start(bias_rows[HEADS:HEADS + KVH, :], bkv[0:KVH * HD].rearrange("(h d) -> h d", d=HD))\
           .then_inc(bias_ld, 16)
        act.dma_start(ffn_raw[:, :, :], W_base.rearrange("(c p) n -> p c n", p=P)).then_inc(ffn_ld, 16)
        act.dma_start(A_raw[:, :], A_stack.rearrange("e r n -> (e r) n")).then_inc(ffn_ld, 16)
        act.dma_start(R_raw[:, :], W_router).then_inc(ffn_ld, 16)
        for c in range(DC):
            act.dma_start(B_raw[:, c, :].rearrange("p (e r) -> p e r", r=RANK),
                          B_stack[:, c * P:(c + 1) * P, :].rearrange("e p r -> p e r")).then_inc(ffn_ld, 16)

        act.dma_start(bv_bc[:, :], bkv[KVH * HD:2 * KVH * HD].partition_broadcast(P)).then_inc(bv_ld, 16)

        act.wait_ge(b_mm, 1)
        act.activation(bqT[:, :], bank(4, HEADS), ACT.Copy, scale=SCALE).then_inc(b_rdy, 1)
        act.activation(bkT[:, :], bank(4)[:, HEADS:HEADS + KVH], ACT.Copy).then_inc(b_rdy, 1)
        for t in range(NT):
            act.wait_ge(xT_mm, t + 1)
            act.activation(xT[0][:, :, t * P:(t + 1) * P],
                           bank(6 + t % 2).rearrange("p (k t) -> p k t", k=DC), ACT.Copy)\
               .then_inc(xT_hi_s, 1)
        for k in range(DC):
            need(act, wkv_split, 2 * k)
            act.dma_start(wkv_raw[0][:, :], WKV_V[k]).then_inc(wkv_ld, 16)
            act.wait_ge(wkv_ld, 16 * (k + 1))
            act.activation(wk[0][:, k, :], wkv_raw[0][:, 0:KVH * HD], ACT.Copy).then_inc(wkv_hi_s, 1)
            act.activation(wv[0][:, k, :], wkv_raw[0][:, KVH * HD:], ACT.Copy).then_inc(wkv_hi_s, 1)
        def ctx_hi(b, kt):
            n = keys_in(kt)
            act.wait_ge(c_t, KT * b + kt + 1)
            act.activation(ctxT[0][:, :, kt * P:kt * P + n],
                           bank(6 + kt % 2).rearrange("p (k t) -> p k t", k=DC)[:, :, 0:n], ACT.Copy)\
               .then_inc(c_hi, 1)

        def kv_round(b, first):
            for kt in range(KT):
                ctx_hi(b, kt)
            for h in range(KVH):
                if not first or h >= 2:
                    act.wait_ge(k_st[h % 2], 16 * (4 * b + h // 2))
                for c, (at, _, valid) in enumerate(CHUNKS):
                    act.wait_ge(k_mm, 4 * (KVH * b + h) + c + 1)
                    act.activation(k_stage[h % 2][:, at:at + valid], bank(c, valid), ACT.Identity,
                                   bias=bkT[:, h:h + 1]).then_inc(k_ev, 1)

        for i in range(2):
            act.wait_ge(q_st[i], 16 * HEADS // 2)
        kv_round(0, True)
        with act.Fori(1, BATCH) as b:
            kv_round(b, False)

        act.wait_ge(v_mm, 2 * KT * BATCH)

        def a_step(n, s, has_s, has_m):
            m = n - 1
            par = s % 2
            for kind, i in ACT_UNITS:
                if kind == "T" and has_m:
                    act.wait_ge(t_mm, (KT + 1) * m + i + 1)
                    if i < KT:
                        rows_n = keys_in(i)
                        need(act, pv_mm, KT * m + (i - 2 if i else 0))
                        act.activation(pT[i % 3][0][0:rows_n, :], bank(4 + i % 2)[0:rows_n, :], ACT.Copy)\
                           .then_inc(pt_hi, 1)
                    else:
                        need(act, o_nrm, m)
                        act.activation(r_bc[:, :], bank(4 + i % 2), ACT.Copy).then_inc(r_cp, 1)
                elif kind == "E" and has_s:
                    if i == 0 and (not isinstance(n, int) or n >= 2):
                        act.wait_ge(t_mm, (KT + 1) * (n - 1))
                        act.wait_ge(rs_s, n - 1)
                    act.wait_ge(nm_s, 4 * n + i + 1)
                    act.activation(prob[par][i][:, 0:3 * CW].rearrange("p (c n) -> p c n", c=3),
                                   psum[:, 0:3 * BANK].rearrange("p (c n) -> p c n", c=3)[:, :, 0:CW],
                                   ACT.Exp, bias=nmax[:, i % 2, :], accum_out=rows[:, par, i, 0:1])\
                       .then_inc(ex_a, 1)
                elif kind == "F" and has_s:
                    act.activation(prob[par][i][:, 3 * CW:KEYS], bank(3, KEYS - 3 * CW), ACT.Exp,
                                   bias=nmax[:, i % 2, :], accum_out=rows[:, par, i, 1:2])\
                       .then_inc(ex_b, 1)
                elif kind == "N" and has_m:
                    act.wait_ge(o_nrm, m + 1)
                    need(act, o_mm, 2 * m)
                    act.activation(oT[0][:, :], o_f[:, :], ACT.Copy).then_inc(o_hi_s, 1)

        for s in range(PG):
            a_step(s, s, True, s > 0)
        with act.Fori(1, KVH) as g:
            for s in range(PG):
                a_step(PG * g + s, s, True, True)
        a_step(NSTEP, 0, False, True)

        act.wait_ge(fx_ld, 80)
        act.activation(tg[:, :], gates[:, :], ACT.Tanh).then_inc(g_rdy, 1)
        for t in range(NT + 2):
            if t < NT:
                p = t % 2
                act.wait_ge(f_tr, t + 1)
                act.activation(f_xT[p][:, :, :].rearrange("p k t -> p (k t)"), bank(5 + p), ACT.Copy)\
                   .then_inc(f_xT_s, 1)
            if 1 <= t <= NT:
                u = t - 1
                p = u % 2
                act.wait_ge(f_nm, u + 1)
                act.activation(f_sm[p][:, 8:16], bank(p, EXPERTS), ACT.Exp, bias=f_sm[p][:, 0:1],
                               accum_out=f_sm[p][:, 1:2]).then_inc(f_ex, 1)
                act.wait_ge(f_ht, u + 1)
                act.activation(f_hT[p][:, :], bank(7, P), ACT.Copy).then_inc(f_hT_s, 1)

    @block.vector
    def _(dve):
        for i in range(2):
            dve.wait_ge(x_ld[i], 16)
            for t in range(4 * i, 4 * i + 4):
                dve.bn_stats(stats[:, t, :], xn[:, t, :]).then_inc(x_stat, 1)
            for t in range(4 * i, 4 * i + 4):
                dve.wait_ge(x_stat, 5 * i + 4 * i + 4 if i else 4)
                dve.bn_aggr(mv[:, t, :], stats[:, t, :]).then_inc(x_stat, 1)
            dve.wait_ge(x_stat, 9 * i + 8)
            dve.tensor_scalar(veps[:, 4 * i:4 * i + 4], mv[:, 4 * i:4 * i + 4, 1], EPS, None, ALU.add)\
               .then_inc(x_var, 1)
            dve.wait_ge(x_var, i + 1)
            if i == 0:
                dve.sem_inc(x_stat, 1)

        def xt_lo(t):
            dve.wait_ge(xT_hi_s, t + 1)
            sl = slice(t * P, (t + 1) * P)
            dve.tensor_tensor(xT[1][:, :, sl], bank(6 + t % 2).rearrange("p (k t) -> p k t", k=DC),
                              f32(xT[0][:, :, sl]), ALU.subtract).then_inc(xT_lo_s, 1)

        for t in range(NT):
            dve.wait_ge(x_rstd, t // 4 + 1)
            dve.tensor_scalar(xn[:, t, :], xn[:, t, :], mv[:, t, 0:1], rstd[:, t:t + 1],
                              ALU.subtract, ALU.mult).then_inc(xn_rdy, 1)
            if t >= 2:
                xt_lo(t - 2)
        for t in range(NT - 2, NT):
            xt_lo(t)

        def q_round(g, first):
            for hh in range(GQ):
                h = GQ * g + hh
                if not first or hh >= 2:
                    dve.wait_ge(q_st[hh % 2], 16 * (2 * g + hh // 2))
                for half in range(2):
                    dve.wait_ge(q_mm, 2 * h + half + 1)
                    dve.tensor_scalar(q_stage[hh % 2][:, half * BANK:(half + 1) * BANK],
                                      bank((hh % 2) * 2 + half), SCALE,
                                      bqT[:, bass.ds(GQ * g + hh, 1)], ALU.mult, ALU.add)\
                       .then_inc(q_ev, 1)

        dve.wait_ge(b_rdy, 2)
        q_round(0, True)
        for k in range(DC):
            for i, (hi, lo) in enumerate((wk, wv)):
                dve.wait_ge(wkv_hi_s, 2 * k + i + 1)
                dve.tensor_tensor(lo[:, k, :], wkv_raw[0][:, i * KVH * HD:(i + 1) * KVH * HD],
                                  f32(hi[:, k, :]), ALU.subtract).then_inc(wkv_split, 1)
        with dve.Fori(1, KVH) as g:
            q_round(g, False)
        for n in range(FFN_GROUPS):
            dve.wait_ge(f_mm, n + 1)
            src, dst = ffn_piece(n)
            dve.tensor_copy(dst, bank(4 + n % 2)[0:src[1], 0:src[2]]).then_inc(f_ev, 1)

        for i in range(2):
            dve.wait_ge(q_st[i], 16 * HEADS // 2)
        dve.memset(f32(ctxT[0][:, :, KEYS:KEYS_E]), 0.0).then_inc(pad, 1)
        dve.memset(f32(ctxT[1][:, :, KEYS:KEYS_E]), 0.0).then_inc(pad, 1)
        dve.wait_ge(bv_ld, 16)

        def ctx_lo(b, kt):
            n = keys_in(kt)
            sl = slice(kt * P, kt * P + n)
            dve.wait_ge(c_hi, KT * b + kt + 1)
            dve.tensor_tensor(ctxT[1][:, :, sl],
                              bank(6 + kt % 2).rearrange("p (k t) -> p k t", k=DC)[:, :, 0:n],
                              f32(ctxT[0][:, :, sl]), ALU.subtract).then_inc(c_lo, 1)

        def v_evac(b, kt, first):
            n = keys_in(kt)
            if not first or kt >= 2:
                dve.wait_ge(v_st[kt % 2], 16 * ((KT + 1 - kt % 2) // 2 * b + kt // 2))
            for half in range(2):
                sl = slice(half * BANK, (half + 1) * BANK)
                dve.wait_ge(v_mm, 2 * (KT * b + kt) + half + 1)
                dve.tensor_tensor(v_stage[kt % 2][0:n, sl], bank(4 + half)[0:n, :], bv_bc[0:n, sl],
                                  ALU.add).then_inc(v_ev, 1)

        for kt in range(KT):
            ctx_lo(0, kt)
        for kt in range(KT):
            v_evac(0, kt, True)
            ctx_lo(1, kt)
        with dve.Fori(2, BATCH) as b:
            for kt in range(KT):
                v_evac(b - 1, kt, False)
                ctx_lo(b, kt)
        for kt in range(KT):
            v_evac(BATCH - 1, kt, False)

        def a_step(n, s, has_s, has_m, has_o):
            m = n - 1
            par = s % 2
            for kind, i in DVE_UNITS:
                if kind == "A" and has_o:
                    mo = n - 2
                    t = 2 * (((s - 2) % PG) // 2) + i
                    dve.wait_ge(o_mm, 2 * mo + i + 1)
                    need(dve, o_add, 2 * (mo - 1) + i + 1)
                    dve.tensor_tensor(acc[:, t, :], bank(7 - i), acc[:, t, :], ALU.add)\
                       .then_inc(o_add, 1)
                elif kind == "I" and has_m:
                    dve.wait_ge(ex_b, 4 * (m + 1))
                    dve.tensor_tensor(rsum[:, :], rows[:, 1 - par, :, 0], rows[:, 1 - par, :, 1],
                                      ALU.add).then_inc(rs_s, 1)
                    dve.wait_ge(rs_s, m + 1)
                    need(dve, t_mm, (KT + 1) * m)
                    dve.reciprocal(rinv[:, :], rsum[:, :]).then_inc(ri_s, 1)
                elif kind == "T" and has_m:
                    rows_n = keys_in(i)
                    dve.wait_ge(pt_hi, KT * m + i + 1)
                    dve.tensor_tensor(pT[i % 3][1][0:rows_n, :], bank(4 + i % 2)[0:rows_n, :],
                                      f32(pT[i % 3][0][0:rows_n, :]), ALU.subtract).then_inc(pt_lo, 1)
                elif kind == "N" and has_m:
                    dve.wait_ge(pv_mm, KT * (m + 1))
                    dve.wait_ge(r_cp, m + 1)
                    need(dve, o_split, m)
                    dve.tensor_tensor(o_f[:, :], bank(6), r_bc[:, :], ALU.mult).then_inc(o_nrm, 1)
                elif kind == "L" and has_m:
                    dve.wait_ge(o_hi_s, m + 1)
                    dve.tensor_tensor(oT[1][:, :], o_f[:, :], f32(oT[0][:, :]), ALU.subtract)\
                       .then_inc(o_split, 1)
                elif kind == "M" and has_s:
                    qt, part = i // 4, i % 4
                    q = 4 * n + qt
                    if part == 0:
                        need(dve, nm_s, q - 1)
                        dve.wait_ge(s_mm, 3 * q + 1)
                        dve.tensor_reduce(mx[:, qt % 2, 0:1],
                                          psum[:, 0:2 * BANK].rearrange("p (c n) -> p c n", c=2)[:, :, 0:CW],
                                          AX.XY, ALU.max).then_inc(mx_s, 1)
                    elif part < 3:
                        c = part + 1
                        dve.wait_ge(s_mm, 3 * q + c)
                        dve.tensor_reduce(mx[:, qt % 2, part:part + 1], bank(c, CHUNKS[c][2]), AX.X,
                                          ALU.max).then_inc(mx_s, 1)
                    else:
                        dve.wait_ge(mx_s, 3 * q + 3)
                        need(dve, ex_b, q - 1)
                        dve.tensor_reduce(nmax[:, qt % 2, :], mx[:, qt % 2, :], AX.X, ALU.max,
                                          negate=True).then_inc(nm_s, 1)

        dve.wait_ge(acc_0, 1)
        for s in range(PG):
            a_step(s, s, True, s > 0, s > 1)
        with dve.Fori(1, KVH) as g:
            for s in range(PG):
                a_step(PG * g + s, s, True, True, True)
        a_step(NSTEP, 0, False, True, True)
        a_step(NSTEP + 1, 1, False, False, True)

        count = [0]

        def step(ins):
            count[0] += 1
            ins.then_inc(fv, 1)
            dve.wait_ge(fv, count[0])

        dve.wait_ge(o_add, 2 * NSTEP)
        dve.wait_ge(fx_ld, 80)
        dve.wait_ge(g_rdy, 2)
        for t in range(NT + 2):
            if t < NT:
                p = t % 2
                x1 = f_x1[t % 4]
                step(dve.tensor_tensor(f_y[p][:, :], acc[:, t, :], bo_bc[:, :], ALU.add))
                step(dve.scalar_tensor_tensor(x1[:, :], f_y[p][:, :], tg[:, 0:1], xr[:, t, :],
                                              ALU.mult, ALU.add))
                step(dve.bn_stats(stats[:, t, :], x1[:, :]))
                step(dve.bn_aggr(mv[:, t, :], stats[:, t, :]))
                dve.tensor_scalar(veps[:, t:t + 1], mv[:, t, 1:2], EPS, None, ALU.add).then_inc(f_var, 1)
                dve.wait_ge(f_rstd, t + 1)
                need(dve, f_tr, t - 1)
                dve.tensor_scalar(f_xn[p][:, :], x1[:, :], mv[:, t, 0:1], rstd[:, t:t + 1],
                                  ALU.subtract, ALU.mult).then_inc(f_xn_s, 1)
            if 1 <= t <= NT:
                u = t - 1
                p = u % 2
                sm = f_sm[p]
                pa = bank(p, EXPERTS + P)
                dve.wait_ge(f_ra, u + 1)
                dve.tensor_reduce(sm[:, 0:1], pa[:, 0:EXPERTS], AX.X, ALU.max, negate=True).then_inc(f_nm, 1)
                dve.wait_ge(f_ex, u + 1)
                step(dve.reciprocal(sm[:, 2:3], sm[:, 1:2]))
                step(dve.tensor_scalar(sm[:, 16:24], sm[:, 8:16], sm[:, 2:3], None, ALU.mult))
                step(dve.max(sm[:, 24:32], sm[:, 16:24]))
                step(dve.max_index(f_ix[p][:, :], sm[:, 24:32], sm[:, 16:24]))
                step(dve.tensor_copy(sm[:, 32:34], f_ix[p][:, 0:2]))
                step(dve.tensor_tensor(sm[:, 3:4], sm[:, 24:25], sm[:, 25:26], ALU.add))
                step(dve.reciprocal(sm[:, 4:5], sm[:, 3:4]))
                step(dve.tensor_scalar(sm[:, 34:36], sm[:, 24:26], sm[:, 4:5], LORA_SCALE,
                                       ALU.mult, ALU.mult))
                step(dve.tensor_scalar(sm[:, 40:48], iota_e[:, :], sm[:, 32:33], sm[:, 34:35],
                                       ALU.is_equal, ALU.mult))
                step(dve.tensor_scalar(sm[:, 48:56], iota_e[:, :], sm[:, 33:34], sm[:, 35:36],
                                       ALU.is_equal, ALU.mult))
                step(dve.tensor_tensor(sm[:, 56:64], sm[:, 40:48], sm[:, 48:56], ALU.add))
                need(dve, f_ht, u - 1)
                dve.tensor_tensor(f_hc[p][:, :].rearrange("p (e r) -> p e r", r=RANK),
                                  pa[:, EXPERTS:EXPERTS + P].rearrange("p (e r) -> p e r", r=RANK),
                                  sm[:, 56:64].unsqueeze(2).to_broadcast([P, EXPERTS, RANK]),
                                  ALU.mult).then_inc(f_hc_s, 1)
            if t >= 2:
                u = t - 2
                p = u % 2
                dve.wait_ge(f_out, u + 1)
                step(dve.tensor_tensor(f_y[p][:, :], bank(2 + u % 3), bb_bc[:, :], ALU.add))
                if u >= 2:
                    dve.wait_ge(f_st[p], 16 * (u // 2))
                dve.scalar_tensor_tensor(f_o[p][:, :], f_y[p][:, :], tg[:, 1:2], f_x1[u % 4][:, :],
                                         ALU.mult, ALU.add).then_inc(f_fin, 1)
                dve.wait_ge(f_fin, u + 1)

    @block.tensor
    def _(pe):
        pe.wait_ge(id_rdy, 2)
        pe.wait_ge(bias_ld, 32)
        nb = HEADS + KVH
        nc.tensor.transpose(bank(4, nb), bias_rows[:, :], ident[0:nb, 0:nb]).then_inc(b_mm, 1)
        for t in range(NT):
            pe.wait_ge(xn_rdy, t + 1)
            need(pe, xT_lo_s, t - 1)
            for k in range(DC):
                last = nc.tensor.transpose(bank(6 + t % 2)[:, k * P:(k + 1) * P],
                                           xn[:, t, k * P:(k + 1) * P], ident[:, :])
            last.then_inc(xT_mm, 1)
        pe.wait_ge(xT_lo_s, NT)

        def q_round(g, first):
            for hh in range(GQ):
                h = GQ * g + hh
                pe.wait_ge(wq_split, h + 1)
                for half in range(2):
                    if not first or hh >= 2:
                        pe.wait_ge(q_ev, 2 * h + half - 3)
                    sl = slice(half * BANK, (half + 1) * BANK)
                    for k in range(DC):
                        last = product(bank((hh % 2) * 2 + half),
                                       [w[:, k, :] for w in wq[hh]], [a[:, k, sl] for a in xT],
                                       k == 0, k == DC - 1)
                    last.then_inc(q_mm, 1)

        q_round(0, True)
        with pe.Fori(1, KVH) as g:
            q_round(g, False)

        pe.wait_ge(ffn_ld, 16 * (3 + DC))
        pe.wait_ge(b_rdy, 2)
        for n in range(FFN_GROUPS):
            need(pe, f_ev, n - 1)
            (src, ro, co), _ = ffn_piece(n)
            nc.tensor.transpose(bank(4 + n % 2)[0:ro, 0:co], src, ident[0:co, 0:co]).then_inc(f_mm, 1)
        pe.wait_ge(f_ev, FFN_GROUPS)

        def ctx_t(b, kt, first):
            n = keys_in(kt)
            if kt == 0:
                pe.wait_ge(ctx_ld, 16 * (b + 1))
            if kt == KT - 1:
                pe.wait_ge(ctx_tail_ld, 16 * (b + 1))
            if not first or kt >= 2:
                pe.wait_ge(c_lo, KT * b + (kt - 1 if kt else 0))
            for k in range(DC):
                last = nc.tensor.transpose(bank(6 + kt % 2)[:, k * P:k * P + n],
                                           ctx_raw[0:n, kt, k * P:(k + 1) * P], ident[0:n, 0:n])
            last.then_inc(c_t, 1)

        def v_tile(b, kt, first):
            n = keys_in(kt)
            for half in range(2):
                if not first or kt >= 1:
                    pe.wait_ge(v_ev, 2 * (KT * b + kt) + half - 1)
                cols = slice(half * BANK, (half + 1) * BANK)
                for k in range(DC):
                    last = product(bank(4 + half)[0:n, :],
                                   [a[:, k, kt * P:kt * P + n] for a in ctxT],
                                   [w[:, k, cols] for w in wv], k == 0, k == DC - 1)
                last.then_inc(v_mm, 1)

        def k_heads(b, first):
            pe.wait_ge(c_lo, KT * (b + 1))
            for h in range(KVH):
                for c, (at, w_, _) in enumerate(CHUNKS):
                    if not first or h >= 1:
                        pe.wait_ge(k_ev, 4 * (KVH * b + h) + c - 3)
                    for k in range(DC):
                        last = product(bank(c, w_), [w[:, k, h * HD:(h + 1) * HD] for w in wk],
                                       [a[:, k, at:at + w_] for a in ctxT], k == 0, k == DC - 1)
                    last.then_inc(k_mm, 1)

        for kt in range(KT):
            ctx_t(0, kt, True)
        pe.wait_ge(wkv_split, 2 * DC)
        pe.wait_ge(pad, 2)
        pe.wait_ge(q_ev, 2 * HEADS)
        k_heads(0, True)
        for kt in range(KT):
            v_tile(0, kt, True)
            ctx_t(1, kt, False)
        k_heads(1, False)
        with pe.Fori(2, BATCH) as b:
            for kt in range(KT):
                v_tile(b - 1, kt, False)
                ctx_t(b, kt, False)
            k_heads(b, False)
        for kt in range(KT):
            v_tile(BATCH - 1, kt, False)

        def a_step(g, n, s, has_s, has_m, has_o):
            m = n - 1
            i_m = ((s - 1) % PG) // 2
            for unit in PE_UNITS:
                if unit[0] == "O" and has_o:
                    tt = unit[1]
                    mo = n - 2
                    j = s % 2
                    if tt == 0:
                        pe.wait_ge(o_split, mo + 1)
                        pe.wait_ge(wo_split, (g if s >= 2 else g - 1) + 1)
                    need(pe, o_add, 2 * mo if tt == 0 else 2 * mo)
                    for hh in range(2):
                        at = hh * TOK + tt * P
                        last = product(bank(7 if tt == 0 else 6), [o[:, at:at + P] for o in oT],
                                       [w[:, 2 * j + hh, :] for w in wo], hh == 0, hh == 1)
                    last.then_inc(o_mm, 1)
                elif unit[0] == "T" and has_m:
                    u = unit[1]
                    if u == 0:
                        pe.wait_ge(ex_b, 4 * (m + 1))
                    if u == 1:
                        need(pe, r_cp, m)
                    elif u == 0:
                        need(pe, pt_lo, KT * m)
                    else:
                        pe.wait_ge(pt_lo, KT * m + u - 1)
                    if u == KT:
                        pe.wait_ge(ri_s, m + 1)
                    for qt in range(4):
                        n_out = keys_in(u) if u < KT else P
                        src = (prob[1 - s % 2][qt][:, u * P:u * P + n_out] if u < KT
                               else rinv[:, qt:qt + 1].to_broadcast([P, P]))
                        last = nc.tensor.transpose(bank(4 + u % 2)[0:n_out, qt * P:(qt + 1) * P], src,
                                                   ident[:, :])
                    last.then_inc(t_mm, 1)
                elif unit[0] == "P" and has_m:
                    kt = unit[1]
                    n_k = keys_in(kt)
                    pe.wait_ge(pt_lo, KT * m + kt + 1)
                    if kt == 0:
                        need(pe, o_add, 2 * m)
                        pe.wait_ge(v_split, BATCH * (g if s >= 1 else g - 1) + i_m + 1)
                    product(bank(6), [v[0:n_k, kt, :] for v in vh[i_m % 2]],
                            [t[0:n_k, :] for t in pT[kt % 3]], kt == 0, kt == KT - 1)\
                        .then_inc(pv_mm, 1)
                elif unit[0] == "S" and has_s:
                    qt, c = unit[1:]
                    q = 4 * n + qt
                    b = s // 2
                    if qt == 0 and c == 0:
                        pe.wait_ge(k_split, BATCH * g + b + 1)
                        pe.wait_ge(q_split, n + 1)
                    if c == 0:
                        need(pe, ex_a, q)
                    if c == 3:
                        need(pe, ex_b, q)
                    at, w_, _ = CHUNKS[c]
                    hh, tt = qt // 2, qt % 2
                    col = hh * TOK + tt * P
                    last = product(bank(c, w_), [a[:, col:col + P] for a in qh[s % 2]],
                                   [a[:, at:at + w_] for a in kh[b % 2]], True, True)
                    if c >= 1:
                        last.then_inc(s_mm, 1)

        pe.wait_ge(pad, 6)
        pe.wait_ge(v_ev, 2 * KT * BATCH)
        for s in range(PG):
            a_step(0, s, s, True, s > 0, s > 1)
        with pe.Fori(1, KVH) as g:
            for s in range(PG):
                a_step(g, PG * g + s, s, True, True, True)
        a_step(KVH, NSTEP, 0, False, True, True)
        a_step(KVH, NSTEP + 1, 1, False, False, True)

        for t in range(NT + 1):
            if t < NT:
                p = t % 2
                pe.wait_ge(f_xn_s, t + 1)
                need(pe, f_xT_s, t - 1)
                if t == 0:
                    pe.wait_ge(o_add, 2 * NSTEP)
                for k in range(DC):
                    last = nc.tensor.transpose(bank(5 + p)[:, k * P:(k + 1) * P],
                                               f_xn[p][:, k * P:(k + 1) * P], ident[:, :])
                last.then_inc(f_tr, 1)
                pe.wait_ge(f_xT_s, t + 1)
                need(pe, f_hc_s, t - 1)
                for k in range(DC):
                    last = nc.tensor.matmul(bank(p, EXPERTS + P), f_xT[p][:, k, :], RAT[:, k, :],
                                            start=k == 0, stop=k == DC - 1)
                last.then_inc(f_ra, 1)
                if t >= 3:
                    pe.wait_ge(f_fin, t - 2)
                for k in range(DC):
                    nc.tensor.matmul(bank(2 + t % 3), f_xT[p][:, k, :], WbT[:, k, :],
                                     start=k == 0, stop=False)
            if t >= 1:
                u = t - 1
                p = u % 2
                pe.wait_ge(f_hc_s, u + 1)
                need(pe, f_hT_s, u)
                nc.tensor.transpose(bank(7, P), f_hc[p][:, :], ident[:, :]).then_inc(f_ht, 1)
                pe.wait_ge(f_hT_s, u + 1)
                nc.tensor.matmul(bank(2 + u % 3), f_hT[p][:, :], BT[:, :], start=False, stop=True)\
                    .then_inc(f_out, 1)

    es.close()


_INS = ["x", "ctx_4096", "g_xattn", "g_ffn", "L0_xattn_Wq", "L0_xattn_bq", "L0_xattn_Wkv",
        "L0_xattn_bkv", "L0_xattn_Wo", "L0_xattn_bo", "L0_ffn_W_base", "L0_ffn_b_base",
        "L0_ffn_W_router", "L0_ffn_A_stack", "L0_ffn_B_stack"]
_OUT = ((4, 256, 512), "float32")


def kernel(**inputs):
    import numpy as _np
    import concourse.bacc as _bacc
    from concourse import mybir as _mybir
    from concourse.bass_utils import run_bass_kernel_spmd as _run

    nc = _bacc.Bacc("TRN2", target_bir_lowering=False, num_devices=1)
    arrays, args = {}, []
    for name in _INS:
        a = _np.ascontiguousarray(inputs[name])
        arrays[f"in_{name}"] = a
        args.append(nc.dram_tensor(f"in_{name}", a.shape, _mybir.dt.from_np(a.dtype), kind="ExternalInput").ap())
    shape, dtype = _OUT
    args.append(nc.dram_tensor("out", shape, _mybir.dt.from_np(_np.dtype(dtype)), kind="ExternalOutput").ap())
    build(nc, *args)
    r = _run(nc, [arrays], core_ids=[0])
    return r.results[0]["out"]
```

```python
import concourse.bass as bass
from concourse import mybir
from contextlib import ExitStack

F32 = mybir.dt.float32
F32R = mybir.dt.float32r
U32 = mybir.dt.uint32
ALU = mybir.AluOpType
ACT = mybir.ActivationFunctionType
AX = mybir.AxisListType

BATCH, TOK, DM = 4, 256, 512
HEADS, KVH, HD = 32, 8, 128
GQ = HEADS // KVH
KEYS = 1601
P = 128
SCALE = float(HD) ** -0.5
EPS = 1e-5
EXPERTS, RANK = 8, 16
LORA_SCALE = 32.0 / RANK

NT = BATCH * TOK // P
DC = DM // P
KT = -(-KEYS // P)
TAIL = KEYS - (KT - 1) * P
KEYS_E = KEYS + KEYS % 2
CW = 402
CHUNKS = [(c * CW, min(CW, KEYS_E - c * CW), min(CW, KEYS - c * CW)) for c in range(4)]
BANK = 512
DMA_SCRATCH = 16640
NSTEP = KVH * BATCH * 2
PG = 8


def keys_in(kt):
    return P if kt < KT - 1 else TAIL


def step_units():
    count = dict(O=0, T=0, P=0, S=0)
    units = []
    for kind in "SSTTSSOTTPPTPPSSTSSTOPTPSSSTSTPPTPTSSSTSPPPTP":
        i = count[kind]
        count[kind] += 1
        units.append(("S", i // 4, i % 4) if kind == "S" else (kind, i))
    return units


def act_units():
    units = []
    count = dict(T=0, E=0, F=0)
    for kind in "TTTTETFTTEFTTTETTFTETFN":
        units.append((kind, count.get(kind, 0)))
        if kind in count:
            count[kind] += 1
    return units


def dve_units():
    units = []
    count = dict(A=0, T=0, M=0)
    for kind in "TTMMMTMTAITMMMMTTTMMMTMTTTMMMMTNAL":
        units.append((kind, count.get(kind, 0)))
        if kind in count:
            count[kind] += 1
    return units


def build(nc, x, ctxt, g_xattn, g_ffn, Wq, bq, Wkv, bkv, Wo, bo, W_base, b_base, W_router,
          A_stack, B_stack, out):
    es = ExitStack()
    q_dram = nc.dram_tensor("q_scratch", (HEADS, P, BATCH * TOK), F32, kind="Internal").ap()
    k_dram = nc.dram_tensor("k_scratch", (BATCH * KVH, P, KEYS), F32, kind="Internal").ap()
    v_dram = nc.dram_tensor("v_scratch", (BATCH * KVH, P, KT * HD), F32, kind="Internal").ap()

    top = [DMA_SCRATCH]

    def sb(name, shape, dt=F32, at=None):
        size = 4
        for s in shape[1:]:
            size *= s
        at = top[0] if at is None else at
        at = -(-at // 32) * 32
        top[0] = at + size
        return nc.alloc_sbuf_tensor_at(name, list(shape), dt, offset=at)

    def sem(name):
        return es.enter_context(nc.semaphore(name))

    ident = sb("ident", [P, P])
    bias_rows = sb("bias_rows", [HEADS + KVH, P])
    bqT = sb("bqT", [P, HEADS])
    bkT = sb("bkT", [P, KVH])
    half_neg = sb("half_neg", [P, NT])
    stats = sb("stats", [P, NT, 6])
    mv = sb("mv", [P, NT, 2])
    veps = sb("veps", [P, NT])
    rstd = sb("rstd", [P, NT])
    WbT = sb("WbT", [P, DC, DM])
    RAT = sb("RAT", [P, DC, EXPERTS + EXPERTS * RANK])
    BT = sb("BT", [EXPERTS * RANK, DM])
    base = top[0]

    wk = [sb("wk_hi", [P, DC, KVH * HD], F32R), sb("wk_lo", [P, DC, KVH * HD], F32R)]
    z_wv = top[0]
    wv = [sb("wv_hi", [P, DC, KVH * HD], F32R), sb("wv_lo", [P, DC, KVH * HD], F32R)]
    z_ctx = top[0]
    ctxT = [sb("ctxT_hi", [P, DC, KEYS_E], F32R), sb("ctxT_lo", [P, DC, KEYS_E], F32R)]
    z_raw = top[0]
    ctx_raw = sb("ctx_raw", [P, KT, DM])
    z_stage = top[0]
    k_stage = [sb(f"k_stage{i}", [P, KEYS]) for i in range(2)]
    v_stage = [sb(f"v_stage{i}", [P, KVH * HD]) for i in range(2)]
    bv_bc = sb("bv_bc", [P, KVH * HD])
    z_end = top[0]

    xT = [sb("xT_hi", [P, DC, BATCH * TOK], F32R, at=z_ctx), sb("xT_lo", [P, DC, BATCH * TOK], F32R)]
    wq_raw = [sb(f"wq_raw{i}", [P, DC, HD]) for i in range(GQ)]
    q_stage = [sb(f"q_stage{i}", [P, BATCH * TOK]) for i in range(2)]
    assert top[0] <= z_raw
    wq = [[sb(f"wq_hi{i}", [P, DC, HD], F32R, at=z_stage if i == 0 else None),
           sb(f"wq_lo{i}", [P, DC, HD], F32R)] for i in range(GQ)]
    assert top[0] <= z_end - 4 * KVH * HD
    xn = sb("xn", [P, NT, DM], at=z_end)
    wkv_raw = [sb(f"wkv_raw{i}", [P, 2 * KVH * HD]) for i in range(1)]
    ffn_raw = sb("ffn_raw", [P, DC, DM], at=z_raw)
    A_raw = sb("A_raw", [P, DM])
    R_raw = sb("R_raw", [EXPERTS, DM])
    B_raw = sb("B_raw", [P, DC, EXPERTS * RANK])

    kh = [[sb(f"k_hi{i}", [P, KEYS_E], F32R, at=base if i == 0 else None),
           sb(f"k_lo{i}", [P, KEYS_E], F32R)] for i in range(2)]
    q_raw = [sb(f"q_raw{i}", [P, 2, TOK]) for i in range(2)]
    assert top[0] <= z_wv
    v1 = [sb("v_hi1", [P, KT, HD], F32R), sb("v_lo1", [P, KT, HD], F32R)]
    pT = [[sb(f"pT_hi{i}", [P, BANK], F32R), sb(f"pT_lo{i}", [P, BANK], F32R)] for i in range(3)]
    r_bc = sb("r_bc", [P, BANK])
    o_f = sb("o_f", [P, BANK])
    oT = [sb("oT_hi", [P, BANK], F32R), sb("oT_lo", [P, BANK], F32R)]
    rows = sb("row_sums", [P, 2, 4, 2])
    rsum = sb("rsum", [P, 4])
    rinv = sb("rinv", [P, 4])
    mx = sb("mx", [P, 2, 3])
    nmax = sb("nmax", [P, 2, 1])
    assert top[0] <= z_ctx
    prob = [[sb(f"prob{i}_{t}", [P, KEYS], at=z_ctx if i + t == 0 else None) for t in range(4)]
            for i in range(2)]
    k_raw = sb("k_raw", [P, KEYS], at=max(top[0], z_raw))
    v_raw = sb("v_raw", [P, KT, HD])
    v0 = [sb("v_hi0", [P, KT, HD], F32R), sb("v_lo0", [P, KT, HD], F32R)]
    vh = [v0, v1]
    wo = [sb("wo_hi", [P, GQ, DM], F32R, at=max(top[0], z_stage)), sb("wo_lo", [P, GQ, DM], F32R)]
    wo_raw = sb("wo_raw", [P, GQ, DM])
    qh = [[sb(f"q_hi{i}", [P, 2 * TOK], F32R, at=max(top[0], z_end) if i == 0 else None),
           sb(f"q_lo{i}", [P, 2 * TOK], F32R)] for i in range(2)]
    acc = sb("acc", [P, NT, DM])

    bb_bc = sb("bb_bc", [P, DM], at=z_ctx)
    gates = sb("gates", [P, 2])
    tg = sb("tanh_gates", [P, 2])
    iota_e = sb("iota_e", [P, EXPERTS])
    xr = sb("x_res", [P, NT, DM])
    assert top[0] <= z_ctx + 4 * 4 * KEYS
    tgbb = sb("tanh_gate_b_base", [P, DM])
    f_x1 = [sb(f"f_x1_{i}", [P, DM]) for i in range(4)]
    f_x1b = [sb(f"f_x1_bias{i}", [P, DM]) for i in range(4)]
    z_f = top[0]
    f_xn = [sb(f"f_xn{i}", [P, DM], at=z_f if i == 0 else None) for i in range(2)]
    f_xT = [sb(f"f_xT{i}", [P, DC, P]) for i in range(2)]
    f_o = [sb(f"f_o{i}", [P, DM]) for i in range(2)]
    f_hc = [sb(f"f_hc{i}", [P, P]) for i in range(2)]
    f_hT = [sb(f"f_hT{i}", [P, P]) for i in range(2)]
    f_sm = [sb(f"f_small{i}", [P, 96]) for i in range(2)]
    f_ix = [sb(f"f_index{i}", [P, 8], U32) for i in range(2)]
    assert top[0] <= z_stage

    psum = es.enter_context(nc.psum_tensor("psum", [P, 8 * BANK], F32))

    def bank(i, w=BANK):
        return psum[:, i * BANK:i * BANK + w]

    x_ld = [sem(f"x_loaded{i}") for i in range(2)]
    wq_ld = [sem(f"wq_loaded{i}") for i in range(GQ)]
    wkv_ld = sem("wkv_loaded")
    bias_ld = sem("bias_loaded")
    bv_ld = sem("bv_loaded")
    ffn_ld = sem("ffn_weights_loaded")
    ctx_ld = sem("ctx_loaded")
    ctx_tail_ld = sem("ctx_tail_loaded")
    id_rdy = sem("ident_ready")
    cst = sem("constants_ready")
    x_stat = sem("x_stats")
    x_var = sem("x_var_ready")
    x_rstd = sem("x_rstd_ready")
    xn_rdy = sem("xn_ready")
    xT_mm = sem("xT_transposed")
    xT_hi_s = sem("xT_hi_ready")
    xT_lo_s = sem("xT_lo_ready")
    b_mm = sem("bias_transposed")
    b_rdy = sem("bias_ready")
    wq_hi_s = sem("wq_hi_ready")
    wq_split = sem("wq_split")
    q_mm = sem("q_multiplied")
    q_ev = sem("q_evacuated")
    q_st = [sem(f"q_stored{i}") for i in range(2)]
    wkv_hi_s = sem("wkv_hi_ready")
    wkv_split = sem("wkv_split")
    f_mm = sem("ffn_weights_transposed")
    f_ev = sem("ffn_weights_evacuated")
    c_t = sem("ctx_transposed")
    c_hi = sem("ctxT_hi_ready")
    c_lo = sem("ctxT_lo_ready")
    k_mm = sem("k_multiplied")
    k_ev = sem("k_evacuated")
    k_st = [sem(f"k_stored{i}") for i in range(2)]
    v_mm = sem("v_multiplied")
    v_ev = sem("v_evacuated")
    v_st = [sem(f"v_stored{i}") for i in range(2)]
    pad = sem("pad_cleared")
    acc_0 = sem("acc_holds_bias")
    split_go = sem("split_may_start")
    k_ld = sem("k_loaded")
    v_ld = sem("v_loaded")
    vt_ld = sem("v_tail_loaded")
    q_ld = [sem(f"q_loaded{i}") for i in range(2)]
    wo_ld = sem("wo_loaded")
    k_hi_s = sem("k_hi_ready")
    k_split = sem("k_split")
    v_hi_s = sem("v_hi_ready")
    v_split = sem("v_split")
    q_hi_s = sem("q_hi_ready")
    q_split = sem("q_split")
    wo_hi_s = sem("wo_hi_ready")
    wo_split = sem("wo_split")
    s_mm = sem("scores_multiplied")
    mx_s = sem("chunk_max_ready")
    nm_s = sem("neg_max_ready")
    ex_a = sem("exp_first_chunks")
    ex_b = sem("exp_last_chunk")
    t_mm = sem("prob_transposed")
    pt_hi = sem("pT_hi_ready")
    pt_lo = sem("pT_lo_ready")
    rs_s = sem("row_sum_ready")
    ri_s = sem("row_inverse_ready")
    r_cp = sem("row_inverse_broadcast")
    pv_mm = sem("pv_multiplied")
    o_nrm = sem("o_normalised")
    o_hi_s = sem("o_hi_ready")
    o_split = sem("o_split")
    o_mm = sem("o_projected")
    o_add = sem("o_accumulated")
    fx_ld = sem("ffn_inputs_loaded")
    g_rdy = sem("gates_ready")
    fv = sem("ffn_vector_steps")
    f_x1_s = sem("ffn_x1_ready")
    f_x1b_s = sem("ffn_x1_bias_ready")
    f_var = sem("ffn_var_ready")
    f_rstd = sem("ffn_rstd_ready")
    f_xn_s = sem("ffn_xn_ready")
    f_tr = sem("ffn_xT_transposed")
    f_xT_s = sem("ffn_xT_ready")
    f_ra = sem("ffn_router_and_a_ready")
    f_bias = sem("ffn_gated_bias_ready")
    f_idx = sem("ffn_top_index_ready")
    f_place = sem("ffn_top_place_ready")
    f_top1 = sem("ffn_top_one_weight_ready")
    f_nm = sem("ffn_router_neg_max")
    f_ex = sem("ffn_router_exp")
    f_hc_s = sem("ffn_expert_hidden_ready")
    f_ht = sem("ffn_hidden_transposed")
    f_hT_s = sem("ffn_hT_ready")
    f_out = sem("ffn_product_ready")
    f_fin = sem("ffn_tile_ready")
    f_st = [sem(f"out_stored{i}") for i in range(2)]

    def need(eng, s, value):
        if isinstance(value, int) and value <= 0:
            return
        eng.wait_ge(s, value)

    def product(o, a, b, first, last):
        nc.tensor.matmul(o, a[1], b[0], start=first, stop=False)
        nc.tensor.matmul(o, a[0], b[1], start=False, stop=False)
        return nc.tensor.matmul(o, a[0], b[0], start=False, stop=last)

    def f32(ap):
        return ap.bitcast(F32)

    WQ_V = Wq.rearrange("(k p) n -> p k n", p=P)
    WKV_V = Wkv.rearrange("(k p) n -> k p n", p=P)
    X_V = x.rearrange("b (t p) n -> p (b t) n", p=P)
    OUT_V = out.rearrange("b (t p) n -> (b t) p n", p=P)
    VB = v_dram.rearrange("(b g) p (t d) -> b p t g d", b=BATCH, d=HD)
    Q_B = q_dram.rearrange("h d (b t) -> h d b t", b=BATCH)
    PE_UNITS, ACT_UNITS, DVE_UNITS = step_units(), act_units(), dve_units()
    FFN_GROUPS = DC + 3

    def ffn_group(n):
        if n < DC:
            return ([ffn_raw[:, n, k * P:(k + 1) * P] for k in range(DC)], P, P,
                    WbT[:, :, n * P:(n + 1) * P])
        if n == DC:
            return ([A_raw[:, k * P:(k + 1) * P] for k in range(DC)], P, P,
                    RAT[:, :, EXPERTS:EXPERTS + P])
        if n == DC + 1:
            return ([R_raw[:, k * P:(k + 1) * P] for k in range(DC)], P, EXPERTS, RAT[:, :, 0:EXPERTS])
        return ([B_raw[:, c, :] for c in range(DC)], P, P, BT[:, :].rearrange("p (c n) -> p c n", c=DC))

    block = es.enter_context(nc.Block())

    @block.sync
    def _(sp):
        for i in range(2):
            sp.dma_start(xn[:, 4 * i:4 * i + 4, :], X_V[:, 4 * i:4 * i + 4, :]).then_inc(x_ld[i], 16)

        def load_wq(g, hh):
            sp.dma_start(wq_raw[hh][:, :, :], WQ_V[:, :, bass.ds(g * GQ * HD + hh * HD, HD)])\
              .then_inc(wq_ld[hh], 16)

        for hh in range(GQ):
            load_wq(0, hh)

        def q_round(g, last):
            for hh in range(GQ):
                if not last:
                    sp.wait_ge(wq_split, GQ * g + hh + 1)
                    load_wq(g + 1, hh)
                sp.wait_ge(q_ev, 2 * (GQ * g + hh) + 2)
                sp.dma_start(q_dram[bass.ds(GQ * g + hh, 1), :, :].rearrange("a p n -> (a p) n"),
                             q_stage[hh % 2][:, :]).then_inc(q_st[hh % 2], 16)

        def load_ctx(b):
            sp.dma_start(ctx_raw[:, 0:KT - 1, :],
                         ctxt[bass.ds(b, 1), 0:(KT - 1) * P, :].rearrange("a (t p) n -> p (a t) n", p=P))\
              .then_inc(ctx_ld, 16)
            sp.dma_start(ctx_raw[0:TAIL, KT - 1, :],
                         ctxt[bass.ds(b, 1), (KT - 1) * P:KEYS, :].rearrange("a p n -> (a p) n"))\
              .then_inc(ctx_tail_ld, 16)

        q_round(0, False)
        sp.wait_ge(f_mm, FFN_GROUPS)
        load_ctx(0)
        with sp.Fori(1, KVH - 1) as g:
            q_round(g, False)
        q_round(KVH - 1, True)

        def store_v(b, kt):
            n = keys_in(kt)
            sp.wait_ge(v_ev, 2 * (KT * b + kt + 1))
            sp.dma_start(VB[bass.ds(b, 1), 0:n, kt, :, :].rearrange("a p g d -> p (a g) d"),
                         v_stage[kt % 2][0:n, :].rearrange("p (g d) -> p g d", d=HD))\
              .then_inc(v_st[kt % 2], 16)

        def kv_round(b, first, last):
            if not first:
                for kt in range(KT):
                    store_v(b - 1, kt)
            if not last:
                sp.wait_ge(c_t, KT * (b + 1))
                load_ctx(b + 1)
            for h in range(KVH):
                sp.wait_ge(k_ev, 4 * (KVH * b + h + 1))
                sp.dma_start(k_dram[bass.ds(b * KVH + h, 1), :, :].rearrange("a p n -> (a p) n"),
                             k_stage[h % 2][:, :]).then_inc(k_st[h % 2], 16)

        kv_round(0, True, False)
        with sp.Fori(1, BATCH - 1) as b:
            kv_round(b, False, False)
        kv_round(BATCH - 1, False, True)
        for i in range(2):
            sp.wait_ge(q_st[i], 16 * HEADS // 2)
            sp.wait_ge(k_st[i], 16 * BATCH * KVH // 2)

        def load_k(i, g, b):
            need(sp, k_split, i)
            sp.dma_start(k_raw[:, :], k_dram[bass.ds(b * KVH + g, 1), :, :].rearrange("a p n -> (a p) n"))\
              .then_inc(k_ld, 16)

        def load_v(i, g, b):
            need(sp, v_split, i)
            src = v_dram[bass.ds(b * KVH + g, 1), :, :].rearrange("a p n -> (a p) n")
            sp.dma_start(v_raw[:, 0:KT - 1, :], src[:, 0:(KT - 1) * HD].rearrange("p (t d) -> p t d", d=HD))\
              .then_inc(v_ld, 16)
            sp.dma_start(v_raw[0:TAIL, KT - 1, :], src[0:TAIL, (KT - 1) * HD:KT * HD]).then_inc(vt_ld, 16)

        def load_q(n, g, b, j):
            need(sp, q_split, n - 1)
            sp.dma_start(q_raw[j][:, :, :],
                         Q_B[bass.ds(GQ * g + 2 * j, 2), :, b, :].rearrange("h d t -> d h t"))\
              .then_inc(q_ld[j], 16)

        def load_wo(g):
            need(sp, wo_split, g)
            sp.dma_start(wo_raw[:, :, :], Wo[bass.ds(g * GQ * HD, GQ * HD), :]
                         .rearrange("(h d) n -> d h n", d=HD)).then_inc(wo_ld, 16)

        def a_loads(g, first):
            for b in range(BATCH):
                i = BATCH * g + b
                load_k(i, g, b)
                load_q(2 * i, g, b, 0)
                if b == 1:
                    load_wo(g)
                load_q(2 * i + 1, g, b, 1)
                if first and b == 0:
                    for kt in range(KT):
                        store_v(BATCH - 1, kt)
                    sp.wait_ge(v_st[0], 16 * BATCH * ((KT + 1) // 2))
                    sp.wait_ge(v_st[1], 16 * BATCH * (KT // 2))
                load_v(i, g, b)

        for t in range(NT):
            sp.dma_start(acc[:, t, :], bo.partition_broadcast(P)).then_inc(acc_0, 16)
        a_loads(0, True)
        with sp.Fori(1, KVH) as g:
            a_loads(g, False)

        sp.wait_ge(t_mm, (KT + 1) * (NSTEP - 1))
        sp.dma_start(gates[:, 0:1], g_xattn.partition_broadcast(P)).then_inc(fx_ld, 16)
        sp.dma_start(gates[:, 1:2], g_ffn.partition_broadcast(P)).then_inc(fx_ld, 16)
        sp.dma_start(xr[:, :, :], X_V).then_inc(fx_ld, 16)
        sp.dma_start(bb_bc[:, :], b_base.partition_broadcast(P)).then_inc(fx_ld, 16)
        for t in range(NT):
            sp.wait_ge(f_fin, t + 1)
            sp.dma_start(OUT_V[t], f_o[t % 2][:, :]).then_inc(f_st[t % 2], 16)
        for i in range(2):
            sp.wait_ge(f_st[i], 16 * NT // 2)

    @block.gpsimd
    def _(pool):
        pool.memset(ident[:, :], 0.0).then_inc(id_rdy, 1)
        pool.memset(half_neg[:, :], -0.5).then_inc(cst, 1)
        pool.wait_ge(id_rdy, 1)
        pool.affine_select(out=ident[:, :], in_=ident[:, :], compare_op=ALU.not_equal, fill=1.0,
                           base=0, pattern=[[-1, P]], channel_multiplier=1).then_inc(id_rdy, 1)
        pool.wait_ge(cst, 1)
        for i in range(2):
            pool.wait_ge(x_var, i + 1)
            sl = slice(4 * i, 4 * i + 4)
            pool.tensor_tensor(rstd[:, sl], veps[:, sl], half_neg[:, sl], ALU.pow).then_inc(x_rstd, 1)

        def split(raw, hi, lo, hi_s, n, split_s):
            pool.sem_inc(split_go, 1)
            pool.tensor_scalar(hi, raw, 1.0, 0.0, ALU.mult, ALU.add).then_inc(hi_s, 1)
            pool.wait_ge(hi_s, n + 1)
            pool.tensor_tensor(lo, raw, f32(hi), ALU.subtract).then_inc(split_s, 1)

        def q_round(g, first):
            for hh in range(GQ):
                h = GQ * g + hh
                pool.wait_ge(wq_ld[hh], 16 * (g + 1))
                if not first:
                    pool.wait_ge(q_mm, 2 * (h - GQ + 1))
                split(wq_raw[hh][:, :, :], wq[hh][0][:, :, :], wq[hh][1][:, :, :], wq_hi_s, h, wq_split)

        q_round(0, True)
        with pool.Fori(1, KVH) as g:
            q_round(g, False)

        pool.wait_ge(k_mm, 4 * BATCH * KVH)
        for i in range(2):
            for part in kh[i]:
                pool.memset(f32(part[:, KEYS:KEYS_E]), 0.0).then_inc(pad, 1)

        def a_splits(g, first):
            for b in range(BATCH):
                i = BATCH * g + b
                pool.wait_ge(k_ld, 16 * (i + 1))
                if not first or i >= 2:
                    pool.wait_ge(s_mm, 24 * (i - 1))
                split(k_raw[:, :], kh[b % 2][0][:, 0:KEYS], kh[b % 2][1][:, 0:KEYS], k_hi_s, i, k_split)
                for j in range(2):
                    n = 2 * i + j
                    if b == 1 and j == 1:
                        pool.wait_ge(wo_ld, 16 * (g + 1))
                        if not first:
                            pool.wait_ge(o_mm, 2 * PG * g)
                        else:
                            pool.wait_ge(v_mm, 2 * KT * BATCH)
                        split(wo_raw[:, :, :], wo[0][:, :, :], wo[1][:, :, :], wo_hi_s, g, wo_split)
                    pool.wait_ge(q_ld[j], 16 * (i + 1))
                    if not first or n >= 2:
                        pool.wait_ge(s_mm, 12 * (n - 1))
                    split(q_raw[j][:, :, :].rearrange("p h t -> p (h t)"), qh[j][0][:, :],
                          qh[j][1][:, :], q_hi_s, n, q_split)
                pool.wait_ge(v_ld, 16 * (i + 1))
                pool.wait_ge(vt_ld, 16 * (i + 1))
                if first and b == 1:
                    pool.wait_ge(v_mm, 2 * KT * BATCH)
                if not first or i >= 2:
                    pool.wait_ge(pv_mm, KT * (2 * i - 2))
                hi, lo = vh[b % 2]
                full = slice(0, KT - 1)
                pool.sem_inc(split_go, 1)
                pool.tensor_scalar(hi[:, full, :], v_raw[:, full, :], 1.0, 0.0, ALU.mult, ALU.add)\
                    .then_inc(v_hi_s, 1)
                pool.tensor_scalar(hi[0:TAIL, KT - 1, :], v_raw[0:TAIL, KT - 1, :], 1.0, 0.0,
                                   ALU.mult, ALU.add).then_inc(v_hi_s, 1)
                pool.wait_ge(v_hi_s, 2 * i + 2)
                pool.tensor_tensor(lo[:, full, :], v_raw[:, full, :], f32(hi[:, full, :]), ALU.subtract)
                pool.tensor_tensor(lo[0:TAIL, KT - 1, :], v_raw[0:TAIL, KT - 1, :],
                                   f32(hi[0:TAIL, KT - 1, :]), ALU.subtract).then_inc(v_split, 1)

        a_splits(0, True)
        with pool.Fori(1, KVH) as g:
            a_splits(g, False)

        pool.wait_ge(t_mm, (KT + 1) * (NSTEP - 1))
        pool.iota(iota_e[:, :], [[1, EXPERTS]], base=0, channel_multiplier=0,
                  allow_small_or_imprecise_dtypes=True).then_inc(g_rdy, 1)
        for t in range(NT):
            pool.wait_ge(f_var, t + 1)
            pool.tensor_tensor(rstd[:, t:t + 1], veps[:, t:t + 1], half_neg[:, t:t + 1], ALU.pow)\
                .then_inc(f_rstd, 1)
            pool.wait_ge(f_x1_s, t + 1)
            if t == 0:
                pool.wait_ge(f_bias, 1)
            need(pool, f_fin, t - 3)
            pool.tensor_tensor(f_x1b[t % 4][:, :], f_x1[t % 4][:, :], tgbb[:, :], ALU.add)\
                .then_inc(f_x1b_s, 1)

    @block.scalar
    def _(act):
        act.dma_start(bias_rows[0:HEADS, :], bq.rearrange("(h d) -> h d", d=HD)).then_inc(bias_ld, 16)
        act.dma_start(bias_rows[HEADS:HEADS + KVH, :], bkv[0:KVH * HD].rearrange("(h d) -> h d", d=HD))\
           .then_inc(bias_ld, 16)
        act.dma_start(ffn_raw[:, :, :], W_base.rearrange("(c p) n -> p c n", p=P)).then_inc(ffn_ld, 16)
        act.dma_start(A_raw[:, :], A_stack.rearrange("e r n -> (e r) n")).then_inc(ffn_ld, 16)
        act.dma_start(R_raw[:, :], W_router).then_inc(ffn_ld, 16)
        for c in range(DC):
            act.dma_start(B_raw[:, c, :].rearrange("p (e r) -> p e r", r=RANK),
                          B_stack[:, c * P:(c + 1) * P, :].rearrange("e p r -> p e r")).then_inc(ffn_ld, 16)

        act.dma_start(bv_bc[:, :], bkv[KVH * HD:2 * KVH * HD].partition_broadcast(P)).then_inc(bv_ld, 16)

        act.wait_ge(b_mm, 1)
        act.activation(bqT[:, :], bank(4, HEADS), ACT.Copy, scale=SCALE).then_inc(b_rdy, 1)
        act.activation(bkT[:, :], bank(4)[:, HEADS:HEADS + KVH], ACT.Copy).then_inc(b_rdy, 1)
        for t in range(NT):
            act.wait_ge(xT_mm, t + 1)
            act.activation(xT[0][:, :, t * P:(t + 1) * P],
                           bank(6 + t % 2).rearrange("p (k t) -> p k t", k=DC), ACT.Copy)\
               .then_inc(xT_hi_s, 1)
        act.dma_start(wkv_raw[0][:, :], WKV_V[0]).then_inc(wkv_ld, 16)
        for n in range(FFN_GROUPS):
            act.wait_ge(f_mm, n + 1)
            _, ro, co, dst = ffn_group(n)
            act.activation(dst, bank(4 + n % 2)[0:ro, :].rearrange("p (k n) -> p k n", k=DC)[:, :, 0:co],
                           ACT.Copy).then_inc(f_ev, 1)
        for k in range(DC):
            if k > 0:
                act.wait_ge(wkv_split, 2 * k)
                act.dma_start(wkv_raw[0][:, :], WKV_V[k]).then_inc(wkv_ld, 16)
            act.wait_ge(wkv_ld, 16 * (k + 1))
            act.activation(wk[0][:, k, :], wkv_raw[0][:, 0:KVH * HD], ACT.Copy).then_inc(wkv_hi_s, 1)
            act.activation(wv[0][:, k, :], wkv_raw[0][:, KVH * HD:], ACT.Copy).then_inc(wkv_hi_s, 1)
        def ctx_hi(b, kt):
            n = keys_in(kt)
            act.wait_ge(c_t, KT * b + kt + 1)
            act.activation(ctxT[0][:, :, kt * P:kt * P + n],
                           bank(6 + kt % 2).rearrange("p (k t) -> p k t", k=DC)[:, :, 0:n], ACT.Copy)\
               .then_inc(c_hi, 1)

        def kv_round(b, first):
            for kt in range(KT):
                ctx_hi(b, kt)
            for h in range(KVH):
                if not first or h >= 2:
                    act.wait_ge(k_st[h % 2], 16 * (4 * b + h // 2))
                for c, (at, _, valid) in enumerate(CHUNKS):
                    act.wait_ge(k_mm, 4 * (KVH * b + h) + c + 1)
                    act.activation(k_stage[h % 2][:, at:at + valid], bank(c, valid), ACT.Identity,
                                   bias=bkT[:, h:h + 1]).then_inc(k_ev, 1)

        for i in range(2):
            act.wait_ge(q_st[i], 16 * HEADS // 2)
        kv_round(0, True)
        with act.Fori(1, BATCH) as b:
            kv_round(b, False)

        act.wait_ge(v_mm, 2 * KT * BATCH)

        def a_step(n, s, has_s, has_m):
            m = n - 1
            par = s % 2
            for kind, i in ACT_UNITS:
                if kind == "T" and has_m:
                    act.wait_ge(t_mm, (KT + 1) * m + i + 1)
                    if i < KT:
                        rows_n = keys_in(i)
                        need(act, pv_mm, KT * m + (i - 2 if i else 0))
                        act.activation(pT[i % 3][0][0:rows_n, :], bank(4 + i % 2)[0:rows_n, :], ACT.Copy)\
                           .then_inc(pt_hi, 1)
                    else:
                        need(act, o_nrm, m)
                        act.activation(r_bc[:, :], bank(4 + i % 2), ACT.Copy).then_inc(r_cp, 1)
                elif kind == "E" and has_s:
                    if i == 0 and (not isinstance(n, int) or n >= 2):
                        act.wait_ge(t_mm, (KT + 1) * (n - 1))
                        act.wait_ge(rs_s, n - 1)
                    act.wait_ge(nm_s, 4 * n + i + 1)
                    act.activation(prob[par][i][:, 0:3 * CW].rearrange("p (c n) -> p c n", c=3),
                                   psum[:, 0:3 * BANK].rearrange("p (c n) -> p c n", c=3)[:, :, 0:CW],
                                   ACT.Exp, bias=nmax[:, i % 2, :], accum_out=rows[:, par, i, 0:1])\
                       .then_inc(ex_a, 1)
                elif kind == "F" and has_s:
                    act.activation(prob[par][i][:, 3 * CW:KEYS], bank(3, KEYS - 3 * CW), ACT.Exp,
                                   bias=nmax[:, i % 2, :], accum_out=rows[:, par, i, 1:2])\
                       .then_inc(ex_b, 1)
                elif kind == "N" and has_m:
                    act.wait_ge(o_nrm, m + 1)
                    need(act, o_mm, 2 * m)
                    act.activation(oT[0][:, :], o_f[:, :], ACT.Copy).then_inc(o_hi_s, 1)

        for s in range(PG):
            a_step(s, s, True, s > 0)
        with act.Fori(1, KVH) as g:
            for s in range(PG):
                a_step(PG * g + s, s, True, True)
        a_step(NSTEP, 0, False, True)

        act.wait_ge(fx_ld, 64)
        act.activation(tg[:, :], gates[:, :], ACT.Tanh).then_inc(g_rdy, 1)

        def xT_copy(t):
            p = t % 2
            act.wait_ge(f_tr, t + 1)
            act.activation(f_xT[p][:, :, :].rearrange("p k t -> p (k t)"), bank(5 + p), ACT.Copy)\
               .then_inc(f_xT_s, 1)

        xT_copy(0)
        xT_copy(1)
        for t in range(1, NT + 1):
            u = t - 1
            p = u % 2
            act.wait_ge(f_nm, u + 1)
            act.activation(f_sm[p][:, 8:16], bank(p, EXPERTS), ACT.Exp, bias=f_sm[p][:, 0:1],
                           accum_out=f_sm[p][:, 1:2]).then_inc(f_ex, 1)
            if t + 1 < NT:
                xT_copy(t + 1)
            act.wait_ge(f_ht, u + 1)
            act.activation(f_hT[p][:, :], bank(7, P), ACT.Copy).then_inc(f_hT_s, 1)

    @block.vector
    def _(dve):
        for i in range(2):
            dve.wait_ge(x_ld[i], 16)
            for t in range(4 * i, 4 * i + 4):
                dve.bn_stats(stats[:, t, :], xn[:, t, :]).then_inc(x_stat, 1)
            for t in range(4 * i, 4 * i + 4):
                dve.wait_ge(x_stat, 5 * i + 4 * i + 4 if i else 4)
                dve.bn_aggr(mv[:, t, :], stats[:, t, :]).then_inc(x_stat, 1)
            dve.wait_ge(x_stat, 9 * i + 8)
            dve.tensor_scalar(veps[:, 4 * i:4 * i + 4], mv[:, 4 * i:4 * i + 4, 1], EPS, None, ALU.add)\
               .then_inc(x_var, 1)
            dve.wait_ge(x_var, i + 1)
            if i == 0:
                dve.sem_inc(x_stat, 1)

        def xt_lo(t):
            dve.wait_ge(xT_hi_s, t + 1)
            sl = slice(t * P, (t + 1) * P)
            dve.tensor_tensor(xT[1][:, :, sl], bank(6 + t % 2).rearrange("p (k t) -> p k t", k=DC),
                              f32(xT[0][:, :, sl]), ALU.subtract).then_inc(xT_lo_s, 1)

        for t in range(NT):
            dve.wait_ge(x_rstd, t // 4 + 1)
            dve.tensor_scalar(xn[:, t, :], xn[:, t, :], mv[:, t, 0:1], rstd[:, t:t + 1],
                              ALU.subtract, ALU.mult).then_inc(xn_rdy, 1)
            if t >= 2:
                xt_lo(t - 2)
        for t in range(NT - 2, NT):
            xt_lo(t)

        def q_round(g, first):
            for hh in range(GQ):
                h = GQ * g + hh
                if not first or hh >= 2:
                    dve.wait_ge(q_st[hh % 2], 16 * (2 * g + hh // 2))
                for half in range(2):
                    dve.wait_ge(q_mm, 2 * h + half + 1)
                    dve.tensor_scalar(q_stage[hh % 2][:, half * BANK:(half + 1) * BANK],
                                      bank((hh % 2) * 2 + half), SCALE,
                                      bqT[:, bass.ds(GQ * g + hh, 1)], ALU.mult, ALU.add)\
                       .then_inc(q_ev, 1)

        dve.wait_ge(b_rdy, 2)
        q_round(0, True)
        for k in range(DC):
            q_round(k + 1, False)
            for i, (hi, lo) in enumerate((wk, wv)):
                dve.wait_ge(wkv_hi_s, 2 * k + i + 1)
                dve.tensor_tensor(lo[:, k, :], wkv_raw[0][:, i * KVH * HD:(i + 1) * KVH * HD],
                                  f32(hi[:, k, :]), ALU.subtract).then_inc(wkv_split, 1)
        with dve.Fori(DC + 1, KVH) as g:
            q_round(g, False)

        for i in range(2):
            dve.wait_ge(q_st[i], 16 * HEADS // 2)
        dve.memset(f32(ctxT[0][:, :, KEYS:KEYS_E]), 0.0).then_inc(pad, 1)
        dve.memset(f32(ctxT[1][:, :, KEYS:KEYS_E]), 0.0).then_inc(pad, 1)
        dve.wait_ge(bv_ld, 16)

        def ctx_lo(b, kt):
            n = keys_in(kt)
            sl = slice(kt * P, kt * P + n)
            dve.wait_ge(c_hi, KT * b + kt + 1)
            dve.tensor_tensor(ctxT[1][:, :, sl],
                              bank(6 + kt % 2).rearrange("p (k t) -> p k t", k=DC)[:, :, 0:n],
                              f32(ctxT[0][:, :, sl]), ALU.subtract).then_inc(c_lo, 1)

        def v_evac(b, kt, first):
            n = keys_in(kt)
            if not first or kt >= 2:
                dve.wait_ge(v_st[kt % 2], 16 * ((KT + 1 - kt % 2) // 2 * b + kt // 2))
            for half in range(2):
                sl = slice(half * BANK, (half + 1) * BANK)
                dve.wait_ge(v_mm, 2 * (KT * b + kt) + half + 1)
                dve.tensor_tensor(v_stage[kt % 2][0:n, sl], bank(4 + half)[0:n, :], bv_bc[0:n, sl],
                                  ALU.add).then_inc(v_ev, 1)

        for kt in range(KT):
            ctx_lo(0, kt)
        for kt in range(KT):
            v_evac(0, kt, True)
            ctx_lo(1, kt)
        with dve.Fori(2, BATCH) as b:
            for kt in range(KT):
                v_evac(b - 1, kt, False)
                ctx_lo(b, kt)
        for kt in range(KT):
            v_evac(BATCH - 1, kt, False)

        def a_step(n, s, has_s, has_m, has_o):
            m = n - 1
            par = s % 2
            for kind, i in DVE_UNITS:
                if kind == "A" and has_o:
                    mo = n - 2
                    t = 2 * (((s - 2) % PG) // 2) + i
                    dve.wait_ge(o_mm, 2 * mo + i + 1)
                    need(dve, o_add, 2 * (mo - 1) + i + 1)
                    dve.tensor_tensor(acc[:, t, :], bank(7), acc[:, t, :], ALU.add)\
                       .then_inc(o_add, 1)
                elif kind == "I" and has_m:
                    dve.wait_ge(ex_b, 4 * (m + 1))
                    dve.tensor_tensor(rsum[:, :], rows[:, 1 - par, :, 0], rows[:, 1 - par, :, 1],
                                      ALU.add).then_inc(rs_s, 1)
                    dve.wait_ge(rs_s, m + 1)
                    need(dve, t_mm, (KT + 1) * m)
                    dve.reciprocal(rinv[:, :], rsum[:, :]).then_inc(ri_s, 1)
                elif kind == "T" and has_m:
                    rows_n = keys_in(i)
                    dve.wait_ge(pt_hi, KT * m + i + 1)
                    dve.tensor_tensor(pT[i % 3][1][0:rows_n, :], bank(4 + i % 2)[0:rows_n, :],
                                      f32(pT[i % 3][0][0:rows_n, :]), ALU.subtract).then_inc(pt_lo, 1)
                elif kind == "N" and has_m:
                    dve.wait_ge(pv_mm, KT * (m + 1))
                    dve.wait_ge(r_cp, m + 1)
                    need(dve, o_split, m)
                    dve.tensor_tensor(o_f[:, :], bank(6), r_bc[:, :], ALU.mult).then_inc(o_nrm, 1)
                elif kind == "L" and has_m:
                    dve.wait_ge(o_hi_s, m + 1)
                    dve.tensor_tensor(oT[1][:, :], o_f[:, :], f32(oT[0][:, :]), ALU.subtract)\
                       .then_inc(o_split, 1)
                elif kind == "M" and has_s:
                    qt, part = i // 4, i % 4
                    q = 4 * n + qt
                    if part == 0:
                        need(dve, nm_s, q - 1)
                        dve.wait_ge(s_mm, 3 * q + 1)
                        dve.tensor_reduce(mx[:, qt % 2, 0:1],
                                          psum[:, 0:2 * BANK].rearrange("p (c n) -> p c n", c=2)[:, :, 0:CW],
                                          AX.XY, ALU.max).then_inc(mx_s, 1)
                    elif part < 3:
                        c = part + 1
                        dve.wait_ge(s_mm, 3 * q + c)
                        dve.tensor_reduce(mx[:, qt % 2, part:part + 1], bank(c, CHUNKS[c][2]), AX.X,
                                          ALU.max).then_inc(mx_s, 1)
                    else:
                        dve.wait_ge(mx_s, 3 * q + 3)
                        need(dve, ex_b, q - 1)
                        dve.tensor_reduce(nmax[:, qt % 2, :], mx[:, qt % 2, :], AX.X, ALU.max,
                                          negate=True).then_inc(nm_s, 1)

        dve.wait_ge(acc_0, 16 * NT)
        for s in range(PG):
            a_step(s, s, True, s > 0, s > 1)
        with dve.Fori(1, KVH) as g:
            for s in range(PG):
                a_step(PG * g + s, s, True, True, True)
        a_step(NSTEP, 0, False, True, True)

        count = [0]

        def step(ins):
            count[0] += 1
            ins.then_inc(fv, 1)
            dve.wait_ge(fv, count[0])

        def norm_stats(t):
            x1 = f_x1[t % 4]
            need(dve, f_x1b_s, t - 3)
            dve.scalar_tensor_tensor(x1[:, :], acc[:, t, :], tg[:, 0:1], xr[:, t, :],
                                     ALU.mult, ALU.add).then_inc(f_x1_s, 1)
            dve.wait_ge(f_x1_s, t + 1)
            step(dve.bn_stats(stats[:, t, :], x1[:, :]))
            step(dve.bn_aggr(mv[:, t, :], stats[:, t, :]))
            dve.tensor_scalar(veps[:, t:t + 1], mv[:, t, 1:2], EPS, None, ALU.add).then_inc(f_var, 1)

        def norm_apply(t):
            dve.wait_ge(f_rstd, t + 1)
            need(dve, f_tr, t - 1)
            dve.tensor_scalar(f_xn[t % 2][:, :], f_x1[t % 4][:, :], mv[:, t, 0:1], rstd[:, t:t + 1],
                              ALU.subtract, ALU.mult).then_inc(f_xn_s, 1)

        def router_max(t):
            dve.wait_ge(f_ra, t + 1)
            dve.tensor_reduce(f_sm[t % 2][:, 0:1], bank(t % 2, EXPERTS), AX.X, ALU.max, negate=True)\
               .then_inc(f_nm, 1)

        def router(t):
            p = t % 2
            sm = f_sm[p]
            dve.wait_ge(f_ex, t + 1)
            step(dve.reciprocal(sm[:, 2:3], sm[:, 1:2]))
            step(dve.tensor_scalar(sm[:, 16:24], sm[:, 8:16], sm[:, 2:3], None, ALU.mult))
            step(dve.max(sm[:, 24:32], sm[:, 16:24]))
            dve.max_index(f_ix[p][:, :], sm[:, 24:32], sm[:, 16:24]).then_inc(f_idx, 1)
            step(dve.tensor_tensor(sm[:, 3:4], sm[:, 24:25], sm[:, 25:26], ALU.add))
            dve.wait_ge(f_idx, t + 1)
            dve.tensor_copy(sm[:, 32:34], f_ix[p][:, 0:2]).then_inc(f_place, 1)
            step(dve.reciprocal(sm[:, 4:5], sm[:, 3:4]))
            step(dve.tensor_scalar(sm[:, 34:36], sm[:, 24:26], sm[:, 4:5], LORA_SCALE,
                                   ALU.mult, ALU.mult))
            dve.wait_ge(f_place, t + 1)
            dve.tensor_scalar(sm[:, 40:48], iota_e[:, :], sm[:, 32:33], sm[:, 34:35],
                              ALU.is_equal, ALU.mult).then_inc(f_top1, 1)
            step(dve.tensor_scalar(sm[:, 48:56], iota_e[:, :], sm[:, 33:34], sm[:, 35:36],
                                   ALU.is_equal, ALU.mult))
            dve.wait_ge(f_top1, t + 1)
            step(dve.tensor_tensor(sm[:, 56:64], sm[:, 40:48], sm[:, 48:56], ALU.add))
            need(dve, f_ht, t - 1)
            dve.tensor_tensor(f_hc[p][:, :].rearrange("p (e r) -> p e r", r=RANK),
                              bank(p, EXPERTS + P)[:, EXPERTS:].rearrange("p (e r) -> p e r", r=RANK),
                              sm[:, 56:64].unsqueeze(2).to_broadcast([P, EXPERTS, RANK]),
                              ALU.mult).then_inc(f_hc_s, 1)

        def finish(t):
            dve.wait_ge(f_out, t + 1)
            dve.wait_ge(f_x1b_s, t + 1)
            if t >= 2:
                dve.wait_ge(f_st[t % 2], 16 * (t // 2))
            dve.scalar_tensor_tensor(f_o[t % 2][:, :], bank(2 + t % 3), tg[:, 1:2], f_x1b[t % 4][:, :],
                                     ALU.mult, ALU.add).then_inc(f_fin, 1)

        dve.wait_ge(fx_ld, 64)
        dve.wait_ge(g_rdy, 2)
        norm_stats(0)
        dve.tensor_scalar(tgbb[:, :], bb_bc[:, :], tg[:, 1:2], None, ALU.mult).then_inc(f_bias, 1)
        norm_apply(0)
        norm_stats(1)
        norm_apply(1)
        a_step(NSTEP + 1, 1, False, False, True)
        dve.wait_ge(o_add, 2 * NSTEP)
        for t in range(1, NT + 2):
            if t + 1 < NT:
                norm_stats(t + 1)
            if t <= NT:
                router_max(t - 1)
            if t + 1 < NT:
                norm_apply(t + 1)
            if t <= NT:
                router(t - 1)
            if t >= 2:
                finish(t - 2)

    @block.tensor
    def _(pe):
        pe.wait_ge(id_rdy, 2)
        pe.wait_ge(bias_ld, 32)
        nb = HEADS + KVH
        nc.tensor.transpose(bank(4, nb), bias_rows[:, :], ident[0:nb, 0:nb]).then_inc(b_mm, 1)
        for t in range(NT):
            pe.wait_ge(xn_rdy, t + 1)
            need(pe, xT_lo_s, t - 1)
            for k in range(DC):
                last = nc.tensor.transpose(bank(6 + t % 2)[:, k * P:(k + 1) * P],
                                           xn[:, t, k * P:(k + 1) * P], ident[:, :])
            last.then_inc(xT_mm, 1)
        pe.wait_ge(xT_lo_s, NT)

        def ffn_transposes(n):
            if n == 0:
                pe.wait_ge(ffn_ld, 16 * (3 + DC))
                pe.wait_ge(b_rdy, 2)
            need(pe, f_ev, n - 1)
            sources, ro, co, _ = ffn_group(n)
            for k, src in enumerate(sources):
                last = nc.tensor.transpose(bank(4 + n % 2)[0:ro, k * P:k * P + co], src,
                                           ident[0:co, 0:co])
            last.then_inc(f_mm, 1)

        def q_round(g, first):
            for hh in range(GQ):
                h = GQ * g + hh
                pe.wait_ge(wq_split, h + 1)
                for half in range(2):
                    if not first or hh >= 2:
                        pe.wait_ge(q_ev, 2 * h + half - 3)
                    sl = slice(half * BANK, (half + 1) * BANK)
                    for k in range(DC):
                        last = product(bank((hh % 2) * 2 + half),
                                       [w[:, k, :] for w in wq[hh]], [a[:, k, sl] for a in xT],
                                       k == 0, k == DC - 1)
                    last.then_inc(q_mm, 1)
                if first:
                    for n in range(2 * hh, min(2 * hh + 2, FFN_GROUPS)):
                        ffn_transposes(n)

        q_round(0, True)
        with pe.Fori(1, KVH) as g:
            q_round(g, False)

        def ctx_t(b, kt, first):
            n = keys_in(kt)
            if kt == 0:
                pe.wait_ge(ctx_ld, 16 * (b + 1))
            if kt == KT - 1:
                pe.wait_ge(ctx_tail_ld, 16 * (b + 1))
            if not first or kt >= 2:
                pe.wait_ge(c_lo, KT * b + (kt - 1 if kt else 0))
            for k in range(DC):
                last = nc.tensor.transpose(bank(6 + kt % 2)[:, k * P:k * P + n],
                                           ctx_raw[0:n, kt, k * P:(k + 1) * P], ident[0:n, 0:n])
            last.then_inc(c_t, 1)

        def v_tile(b, kt, first):
            n = keys_in(kt)
            for half in range(2):
                if not first or kt >= 1:
                    pe.wait_ge(v_ev, 2 * (KT * b + kt) + half - 1)
                cols = slice(half * BANK, (half + 1) * BANK)
                for k in range(DC):
                    last = product(bank(4 + half)[0:n, :],
                                   [a[:, k, kt * P:kt * P + n] for a in ctxT],
                                   [w[:, k, cols] for w in wv], k == 0, k == DC - 1)
                last.then_inc(v_mm, 1)

        def k_chunk(b, h, c, first):
            at, w_, _ = CHUNKS[c]
            if not first:
                pe.wait_ge(k_ev, 4 * (KVH * b + h) + c - 3)
            for k in range(DC):
                last = product(bank(c, w_), [w[:, k, h * HD:(h + 1) * HD] for w in wk],
                               [a[:, k, at:at + w_] for a in ctxT], k == 0, k == DC - 1)
            last.then_inc(k_mm, 1)

        def k_heads(b):
            pe.wait_ge(c_lo, KT * (b + 1))
            for h in range(KVH):
                for c in range(len(CHUNKS)):
                    k_chunk(b, h, c, False)

        done = 0
        for c, (at, w_, valid) in enumerate(CHUNKS):
            tiles = -(-(at + valid) // P)
            for kt in range(done, tiles):
                ctx_t(0, kt, True)
            done = tiles
            if c == 0:
                pe.wait_ge(wkv_split, 2 * DC)
                pe.wait_ge(pad, 2)
                pe.wait_ge(q_ev, 2 * HEADS)
            pe.wait_ge(c_lo, tiles)
            k_chunk(0, 0, c, True)
        for h in range(1, KVH):
            for c in range(len(CHUNKS)):
                k_chunk(0, h, c, False)
        for kt in range(KT):
            v_tile(0, kt, True)
            ctx_t(1, kt, False)
        k_heads(1)
        with pe.Fori(2, BATCH) as b:
            for kt in range(KT):
                v_tile(b - 1, kt, False)
                ctx_t(b, kt, False)
            k_heads(b)
        for kt in range(KT):
            v_tile(BATCH - 1, kt, False)

        def a_step(g, n, s, has_s, has_m, has_o):
            m = n - 1
            i_m = ((s - 1) % PG) // 2
            for unit in PE_UNITS:
                if unit[0] == "O" and has_o:
                    tt = unit[1]
                    mo = n - 2
                    j = s % 2
                    if tt == 0:
                        pe.wait_ge(o_split, mo + 1)
                        pe.wait_ge(wo_split, (g if s >= 2 else g - 1) + 1)
                    need(pe, o_add, 2 * mo + tt)
                    for hh in range(2):
                        at = hh * TOK + tt * P
                        last = product(bank(7), [o[:, at:at + P] for o in oT],
                                       [w[:, 2 * j + hh, :] for w in wo], hh == 0, hh == 1)
                    last.then_inc(o_mm, 1)
                elif unit[0] == "T" and has_m:
                    u = unit[1]
                    if u == 0:
                        pe.wait_ge(ex_b, 4 * (m + 1))
                    if u == 1:
                        need(pe, r_cp, m)
                    elif u == 0:
                        need(pe, pt_lo, KT * m)
                    else:
                        pe.wait_ge(pt_lo, KT * m + u - 1)
                    if u == KT:
                        pe.wait_ge(ri_s, m + 1)
                    for qt in range(4):
                        n_out = keys_in(u) if u < KT else P
                        src = (prob[1 - s % 2][qt][:, u * P:u * P + n_out] if u < KT
                               else rinv[:, qt:qt + 1].to_broadcast([P, P]))
                        last = nc.tensor.transpose(bank(4 + u % 2)[0:n_out, qt * P:(qt + 1) * P], src,
                                                   ident[:, :])
                    last.then_inc(t_mm, 1)
                elif unit[0] == "P" and has_m:
                    kt = unit[1]
                    n_k = keys_in(kt)
                    pe.wait_ge(pt_lo, KT * m + kt + 1)
                    if kt == 0:
                        need(pe, o_nrm, m)
                        pe.wait_ge(v_split, BATCH * (g if s >= 1 else g - 1) + i_m + 1)
                    product(bank(6), [v[0:n_k, kt, :] for v in vh[i_m % 2]],
                            [t[0:n_k, :] for t in pT[kt % 3]], kt == 0, kt == KT - 1)\
                        .then_inc(pv_mm, 1)
                elif unit[0] == "S" and has_s:
                    qt, c = unit[1:]
                    q = 4 * n + qt
                    b = s // 2
                    if qt == 0 and c == 0:
                        pe.wait_ge(k_split, BATCH * g + b + 1)
                        pe.wait_ge(q_split, n + 1)
                    if c == 0:
                        need(pe, ex_a, q)
                    if c == 3:
                        need(pe, ex_b, q)
                    at, w_, _ = CHUNKS[c]
                    hh, tt = qt // 2, qt % 2
                    col = hh * TOK + tt * P
                    last = product(bank(c, w_), [a[:, col:col + P] for a in qh[s % 2]],
                                   [a[:, at:at + w_] for a in kh[b % 2]], True, True)
                    if c >= 1:
                        last.then_inc(s_mm, 1)

        pe.wait_ge(pad, 6)
        pe.wait_ge(v_ev, 2 * KT * BATCH)
        for s in range(PG):
            a_step(0, s, s, True, s > 0, s > 1)
        with pe.Fori(1, KVH) as g:
            for s in range(PG):
                a_step(g, PG * g + s, s, True, True, True)
        a_step(KVH, NSTEP, 0, False, True, True)

        def xn_transposes(t):
            p = t % 2
            pe.wait_ge(f_xn_s, t + 1)
            need(pe, f_xT_s, t - 1)
            for k in range(DC):
                last = nc.tensor.transpose(bank(5 + p)[:, k * P:(k + 1) * P],
                                           f_xn[p][:, k * P:(k + 1) * P], ident[:, :])
            last.then_inc(f_tr, 1)

        def router_and_a(t):
            p = t % 2
            pe.wait_ge(f_xT_s, t + 1)
            need(pe, f_hc_s, t - 1)
            for k in range(DC):
                last = nc.tensor.matmul(bank(p, EXPERTS + P), f_xT[p][:, k, :], RAT[:, k, :],
                                        start=k == 0, stop=k == DC - 1)
            last.then_inc(f_ra, 1)

        def base_layer(t, k):
            if k == 0 and t >= 3:
                pe.wait_ge(f_fin, t - 2)
            nc.tensor.matmul(bank(2 + t % 3), f_xT[t % 2][:, k, :], WbT[:, k, :],
                             start=k == 0, stop=False)

        def hidden_transpose(t):
            pe.wait_ge(f_hc_s, t + 1)
            need(pe, f_hT_s, t)
            nc.tensor.transpose(bank(7, P), f_hc[t % 2][:, :], ident[:, :]).then_inc(f_ht, 1)

        def experts_out(t):
            pe.wait_ge(f_hT_s, t + 1)
            nc.tensor.matmul(bank(2 + t % 3), f_hT[t % 2][:, :], BT[:, :], start=False, stop=True)\
                .then_inc(f_out, 1)

        xn_transposes(0)
        router_and_a(0)
        xn_transposes(1)
        for k in range(DC):
            base_layer(0, k)
        a_step(KVH, NSTEP + 1, 1, False, False, True)
        pe.wait_ge(o_add, 2 * NSTEP)
        for t in range(1, NT + 1):
            if t < NT:
                router_and_a(t)
            if t + 1 < NT:
                xn_transposes(t + 1)
            if t < NT:
                base_layer(t, 0)
                base_layer(t, 1)
            hidden_transpose(t - 1)
            if t < NT:
                base_layer(t, 2)
                base_layer(t, 3)
            experts_out(t - 1)

    es.close()


_INS = ["x", "ctx_4096", "g_xattn", "g_ffn", "L0_xattn_Wq", "L0_xattn_bq", "L0_xattn_Wkv",
        "L0_xattn_bkv", "L0_xattn_Wo", "L0_xattn_bo", "L0_ffn_W_base", "L0_ffn_b_base",
        "L0_ffn_W_router", "L0_ffn_A_stack", "L0_ffn_B_stack"]
_OUT = ((4, 256, 512), "float32")


def kernel(**inputs):
    import numpy as _np
    import concourse.bacc as _bacc
    from concourse import mybir as _mybir
    from concourse.bass_utils import run_bass_kernel_spmd as _run

    nc = _bacc.Bacc("TRN2", target_bir_lowering=False, num_devices=1)
    arrays, args = {}, []
    for name in _INS:
        a = _np.ascontiguousarray(inputs[name])
        arrays[f"in_{name}"] = a
        args.append(nc.dram_tensor(f"in_{name}", a.shape, _mybir.dt.from_np(a.dtype), kind="ExternalInput").ap())
    shape, dtype = _OUT
    args.append(nc.dram_tensor("out", shape, _mybir.dt.from_np(_np.dtype(dtype)), kind="ExternalOutput").ap())
    build(nc, *args)
    r = _run(nc, [arrays], core_ids=[0])
    return r.results[0]["out"]
```

```python
import concourse.bass as bass
from concourse import mybir
from contextlib import ExitStack

F32 = mybir.dt.float32
F32R = mybir.dt.float32r
U32 = mybir.dt.uint32
ALU = mybir.AluOpType
ACT = mybir.ActivationFunctionType
AX = mybir.AxisListType

BATCH, TOK, DM = 4, 256, 512
HEADS, KVH, HD = 32, 8, 128
GQ = HEADS // KVH
KEYS = 1601
P = 128
SCALE = float(HD) ** -0.5
EPS = 1e-5
EXPERTS, RANK = 8, 16
LORA_SCALE = 32.0 / RANK

NT = BATCH * TOK // P
DC = DM // P
KT = -(-KEYS // P)
TAIL = KEYS - (KT - 1) * P
KEYS_E = KEYS + KEYS % 2
CW = 402
CHUNKS = [(c * CW, min(CW, KEYS_E - c * CW), min(CW, KEYS - c * CW)) for c in range(4)]
BANK = 512
DMA_SCRATCH = 16640
NSTEP = KVH * BATCH * 2
PG = 8


def keys_in(kt):
    return P if kt < KT - 1 else TAIL


def step_units():
    count = dict(O=0, T=0, P=0, S=0)
    units = []
    for kind in "SSTTSOSTTPPTPSSSTSPPOTTPSSSTSPTOPTPTSSSTSPPOPP":
        i = count[kind]
        count[kind] += 1
        units.append(("S", i // 4, i % 4) if kind == "S" else (kind, i))
    return units


def act_units():
    units = []
    count = dict(T=0, E=0, F=0, N=0)
    for kind in "TTTETTFTETTFTTETTFTEFN":
        units.append((kind, count[kind]))
        count[kind] += 1
    return units


def dve_units():
    units = []
    count = dict(A=0, I=0, T=0, M=0, L=0)
    for kind in "MTTMMMTIATTMMMMTATTMMMTMTATTMMMMTAL":
        units.append((kind, count[kind]))
        count[kind] += 1
    return units


def build(nc, x, ctxt, g_xattn, g_ffn, Wq, bq, Wkv, bkv, Wo, bo, W_base, b_base, W_router,
          A_stack, B_stack, out):
    es = ExitStack()
    q_dram = nc.dram_tensor("q_scratch", (HEADS, P, BATCH * TOK), F32, kind="Internal").ap()
    k_dram = nc.dram_tensor("k_scratch", (BATCH * KVH, P, KEYS), F32, kind="Internal").ap()
    v_dram = nc.dram_tensor("v_scratch", (BATCH * KVH, P, KT * HD), F32, kind="Internal").ap()

    top = [DMA_SCRATCH]

    def sb(name, shape, dt=F32, at=None):
        size = 4
        for s in shape[1:]:
            size *= s
        at = top[0] if at is None else at
        at = -(-at // 32) * 32
        top[0] = at + size
        return nc.alloc_sbuf_tensor_at(name, list(shape), dt, offset=at)

    def sem(name):
        return es.enter_context(nc.semaphore(name))

    ident = sb("ident", [P, P])
    bias_rows = sb("bias_rows", [HEADS + KVH, P])
    bqT = sb("bqT", [P, HEADS])
    bkT = sb("bkT", [P, KVH])
    half_neg = sb("half_neg", [P, NT])
    stats = sb("stats", [P, NT, 6])
    mv = sb("mv", [P, NT, 2])
    veps = sb("veps", [P, NT])
    rstd = sb("rstd", [P, NT])
    WbT = sb("WbT", [P, DC, DM])
    RAT = sb("RAT", [P, DC, EXPERTS + EXPERTS * RANK])
    BT = sb("BT", [EXPERTS * RANK, DM])
    base = top[0]

    wk = [sb("wk_hi", [P, DC, KVH * HD], F32R), sb("wk_lo", [P, DC, KVH * HD], F32R)]
    z_wv = top[0]
    wv = [sb("wv_hi", [P, DC, KVH * HD], F32R), sb("wv_lo", [P, DC, KVH * HD], F32R)]
    z_ctx = top[0]
    ctxT = [sb("ctxT_hi", [P, DC, KEYS_E], F32R), sb("ctxT_lo", [P, DC, KEYS_E], F32R)]
    z_raw = top[0]
    ctx_raw = sb("ctx_raw", [P, KT, DM])
    z_stage = top[0]
    k_stage = [sb(f"k_stage{i}", [P, KEYS]) for i in range(2)]
    v_stage = [sb(f"v_stage{i}", [P, KVH * HD]) for i in range(2)]
    bv_bc = sb("bv_bc", [P, KVH * HD])
    z_end = top[0]

    xT = [sb("xT_hi", [P, DC, BATCH * TOK], F32R, at=z_ctx), sb("xT_lo", [P, DC, BATCH * TOK], F32R)]
    wq_raw = [sb(f"wq_raw{i}", [P, DC, HD]) for i in range(GQ)]
    assert top[0] <= z_raw
    wq = [[sb(f"wq_hi{i}", [P, DC, HD], F32R, at=z_stage if i == 0 else None),
           sb(f"wq_lo{i}", [P, DC, HD], F32R)] for i in range(GQ)]
    q_stage = [sb("q_stage0", [P, BATCH * TOK])]
    assert top[0] <= z_end - 4 * KVH * HD
    xn = sb("xn", [P, NT, DM], at=z_end)
    wkv_raw = [sb(f"wkv_raw{i}", [P, 2 * KVH * HD]) for i in range(1)]
    q_stage.append(sb("q_stage1", [P, BATCH * TOK]))
    ffn_raw = sb("ffn_raw", [P, DC, DM], at=z_raw)
    A_raw = sb("A_raw", [P, DM])
    R_raw = sb("R_raw", [EXPERTS, DM])
    B_raw = sb("B_raw", [P, DC, EXPERTS * RANK])

    kh = [[sb(f"k_hi{i}", [P, KEYS_E], F32R, at=base if i == 0 else None),
           sb(f"k_lo{i}", [P, KEYS_E], F32R)] for i in range(2)]
    q_raw = [sb(f"q_raw{i}", [P, 2, TOK]) for i in range(2)]
    assert top[0] <= z_wv
    v1 = [sb("v_hi1", [P, KT, HD], F32R), sb("v_lo1", [P, KT, HD], F32R)]
    pT = [[sb(f"pT_hi{i}", [P, BANK], F32R), sb(f"pT_lo{i}", [P, BANK], F32R)] for i in range(3)]
    oT = [sb("oT_hi", [P, BANK], F32R), sb("oT_lo", [P, BANK], F32R)]
    rows = sb("row_sums", [P, 2, 4, 2])
    rsum = sb("rsum", [P, 4])
    rinv = sb("rinv", [P, 2, 4])
    mx = sb("mx", [P, 2, 3])
    nmax = sb("nmax", [P, 2, 1])
    assert top[0] <= z_ctx
    prob = [[sb(f"prob{i}_{t}", [P, KEYS], at=z_ctx if i + t == 0 else None) for t in range(4)]
            for i in range(2)]
    k_raw = sb("k_raw", [P, KEYS], at=max(top[0], z_raw))
    v_raw = sb("v_raw", [P, KT, HD])
    v0 = [sb("v_hi0", [P, KT, HD], F32R), sb("v_lo0", [P, KT, HD], F32R)]
    vh = [v0, v1]
    wo = [sb("wo_hi", [P, GQ, DM], F32R, at=max(top[0], z_stage)), sb("wo_lo", [P, GQ, DM], F32R)]
    wo_raw = sb("wo_raw", [P, GQ, DM])
    qh = [[sb(f"q_hi{i}", [P, 2 * TOK], F32R, at=max(top[0], z_end) if i == 0 else None),
           sb(f"q_lo{i}", [P, 2 * TOK], F32R)] for i in range(2)]
    acc = sb("acc", [P, NT, DM])

    bb_bc = sb("bb_bc", [P, DM], at=z_ctx)
    gates = sb("gates", [P, 2])
    tg = sb("tanh_gates", [P, 2])
    iota_e = sb("iota_e", [P, EXPERTS])
    xr = sb("x_res", [P, NT, DM])
    assert top[0] <= z_ctx + 4 * 4 * KEYS
    tgbb = sb("tanh_gate_b_base", [P, DM])
    f_x1 = [sb(f"f_x1_{i}", [P, DM]) for i in range(4)]
    f_x1b = [sb(f"f_x1_bias{i}", [P, DM]) for i in range(4)]
    z_f = top[0]
    f_xn = [sb(f"f_xn{i}", [P, DM], at=z_f if i == 0 else None) for i in range(2)]
    f_xT = [sb(f"f_xT{i}", [P, DC, P]) for i in range(2)]
    f_o = [sb(f"f_o{i}", [P, DM]) for i in range(2)]
    f_hc = [sb(f"f_hc{i}", [P, P]) for i in range(2)]
    f_hT = [sb(f"f_hT{i}", [P, P]) for i in range(2)]
    f_sm = [sb(f"f_small{i}", [P, 96]) for i in range(2)]
    f_ix = [sb(f"f_index{i}", [P, 8], U32) for i in range(2)]
    assert top[0] <= z_stage

    psum = es.enter_context(nc.psum_tensor("psum", [P, 8 * BANK], F32))

    def bank(i, w=BANK):
        return psum[:, i * BANK:i * BANK + w]

    x_ld = [sem(f"x_loaded{i}") for i in range(NT // 2)]
    wq_ld = [sem(f"wq_loaded{i}") for i in range(GQ)]
    wkv_ld = sem("wkv_loaded")
    bias_ld = sem("bias_loaded")
    bv_ld = sem("bv_loaded")
    ffn_ld = sem("ffn_weights_loaded")
    ctx_ld = sem("ctx_loaded")
    ctx_tail_ld = sem("ctx_tail_loaded")
    id_rdy = sem("ident_ready")
    cst = sem("constants_ready")
    x_stat = sem("x_stats")
    x_var = sem("x_var_ready")
    x_rstd = sem("x_rstd_ready")
    xn_rdy = sem("xn_ready")
    xT_mm = sem("xT_transposed")
    xT_hi_s = sem("xT_hi_ready")
    xT_lo_s = sem("xT_lo_ready")
    b_mm = sem("bias_transposed")
    b_rdy = sem("bias_ready")
    wq_hi_s = sem("wq_hi_ready")
    wq_split = sem("wq_split")
    q_mm = sem("q_multiplied")
    q_ev = sem("q_evacuated")
    q_st = [sem(f"q_stored{i}") for i in range(2)]
    wkv_hi_s = sem("wkv_hi_ready")
    wkv_split = sem("wkv_split")
    f_mm = sem("ffn_weights_transposed")
    f_ev = sem("ffn_weights_evacuated")
    c_t = sem("ctx_transposed")
    c_hi = sem("ctxT_hi_ready")
    c_lo = sem("ctxT_lo_ready")
    k_mm = sem("k_multiplied")
    k_ev = sem("k_evacuated")
    k_st = [sem(f"k_stored{i}") for i in range(2)]
    v_mm = sem("v_multiplied")
    v_ev = sem("v_evacuated")
    v_st = [sem(f"v_stored{i}") for i in range(2)]
    pad = sem("pad_cleared")
    acc_0 = sem("acc_holds_bias")
    split_go = sem("split_may_start")
    k_ld = sem("k_loaded")
    v_ld = sem("v_loaded")
    vt_ld = sem("v_tail_loaded")
    q_ld = [sem(f"q_loaded{i}") for i in range(2)]
    wo_ld = sem("wo_loaded")
    k_hi_s = sem("k_hi_ready")
    k_split = sem("k_split")
    v_hi_s = sem("v_hi_ready")
    v_split = sem("v_split")
    q_hi_s = sem("q_hi_ready")
    q_split = sem("q_split")
    wo_hi_s = sem("wo_hi_ready")
    wo_split = sem("wo_split")
    s_mm = sem("scores_multiplied")
    mx_s = sem("chunk_max_ready")
    nm_s = sem("neg_max_ready")
    ex_a = sem("exp_first_chunks")
    ex_b = sem("exp_last_chunk")
    t_mm = sem("prob_transposed")
    pt_hi = sem("pT_hi_ready")
    pt_lo = sem("pT_lo_ready")
    rs_s = sem("row_sum_ready")
    ri_s = sem("row_inverse_ready")
    pv_mm = sem("pv_multiplied")
    o_hi_s = sem("o_hi_ready")
    o_split = sem("o_split")
    o_mm = sem("o_projected")
    o_add = sem("o_accumulated")
    fx_ld = sem("ffn_inputs_loaded")
    g_rdy = sem("gates_ready")
    fv = sem("ffn_vector_steps")
    f_x1_s = sem("ffn_x1_ready")
    f_x1b_s = sem("ffn_x1_bias_ready")
    f_var = sem("ffn_var_ready")
    f_rstd = sem("ffn_rstd_ready")
    f_xn_s = sem("ffn_xn_ready")
    f_tr = sem("ffn_xT_transposed")
    f_xT_s = sem("ffn_xT_ready")
    f_ra = sem("ffn_router_and_a_ready")
    f_bias = sem("ffn_gated_bias_ready")
    f_idx = sem("ffn_top_index_ready")
    f_place = sem("ffn_top_place_ready")
    f_top1 = sem("ffn_top_one_weight_ready")
    f_nm = sem("ffn_router_neg_max")
    f_ex = sem("ffn_router_exp")
    f_hc_s = sem("ffn_expert_hidden_ready")
    f_ht = sem("ffn_hidden_transposed")
    f_hT_s = sem("ffn_hT_ready")
    f_out = sem("ffn_product_ready")
    f_fin = sem("ffn_tile_ready")
    f_st = [sem(f"out_stored{i}") for i in range(2)]

    def ctx_bank(b, kt):
        return (6, 7, 4, 5)[kt % 4] if isinstance(b, int) and b == 0 else 6 + kt % 2

    def t_bank(kt, s):
        return 4 + (kt + s + 1) % 2

    def need(eng, s, value):
        if isinstance(value, int) and value <= 0:
            return
        eng.wait_ge(s, value)

    def product(o, a, b, first, last):
        nc.tensor.matmul(o, a[1], b[0], start=first, stop=False)
        nc.tensor.matmul(o, a[0], b[1], start=False, stop=False)
        return nc.tensor.matmul(o, a[0], b[0], start=False, stop=last)

    def f32(ap):
        return ap.bitcast(F32)

    WQ_V = Wq.rearrange("(k p) n -> p k n", p=P)
    WKV_V = Wkv.rearrange("(k p) n -> k p n", p=P)
    X_V = x.rearrange("b (t p) n -> p (b t) n", p=P)
    OUT_V = out.rearrange("b (t p) n -> (b t) p n", p=P)
    VB = v_dram.rearrange("(b g) p (t d) -> b p t g d", b=BATCH, d=HD)
    Q_B = q_dram.rearrange("h d (b t) -> h d b t", b=BATCH)
    PE_UNITS, ACT_UNITS, DVE_UNITS = step_units(), act_units(), dve_units()
    FFN_GROUPS = DC + 3

    def ffn_group(n):
        if n < DC:
            return ([ffn_raw[:, n, k * P:(k + 1) * P] for k in range(DC)], P, P,
                    WbT[:, :, n * P:(n + 1) * P])
        if n == DC:
            return ([A_raw[:, k * P:(k + 1) * P] for k in range(DC)], P, P,
                    RAT[:, :, EXPERTS:EXPERTS + P])
        if n == DC + 1:
            return ([R_raw[:, k * P:(k + 1) * P] for k in range(DC)], P, EXPERTS, RAT[:, :, 0:EXPERTS])
        return ([B_raw[:, c, :] for c in range(DC)], P, P, BT[:, :].rearrange("p (c n) -> p c n", c=DC))

    block = es.enter_context(nc.Block())

    @block.sync
    def _(sp):
        for i in range(NT // 2):
            sp.dma_start(xn[:, 2 * i:2 * i + 2, :], X_V[:, 2 * i:2 * i + 2, :]).then_inc(x_ld[i], 16)

        def load_wq(g, hh):
            sp.dma_start(wq_raw[hh][:, :, :], WQ_V[:, :, bass.ds(g * GQ * HD + hh * HD, HD)])\
              .then_inc(wq_ld[hh], 16)

        for hh in range(GQ):
            load_wq(0, hh)

        def q_round(g, last):
            for hh in range(GQ):
                if not last:
                    sp.wait_ge(wq_split, GQ * g + hh + 1)
                    load_wq(g + 1, hh)
                sp.wait_ge(q_ev, 2 * (GQ * g + hh) + 2)
                sp.dma_start(q_dram[bass.ds(GQ * g + hh, 1), :, :].rearrange("a p n -> (a p) n"),
                             q_stage[hh % 2][:, :]).then_inc(q_st[hh % 2], 16)

        def load_ctx(b):
            sp.dma_start(ctx_raw[:, 0:KT - 1, :],
                         ctxt[bass.ds(b, 1), 0:(KT - 1) * P, :].rearrange("a (t p) n -> p (a t) n", p=P))\
              .then_inc(ctx_ld, 16)
            sp.dma_start(ctx_raw[0:TAIL, KT - 1, :],
                         ctxt[bass.ds(b, 1), (KT - 1) * P:KEYS, :].rearrange("a p n -> (a p) n"))\
              .then_inc(ctx_tail_ld, 16)

        q_round(0, False)
        sp.wait_ge(f_mm, FFN_GROUPS)
        load_ctx(0)
        with sp.Fori(1, KVH - 1) as g:
            q_round(g, False)
        q_round(KVH - 1, True)

        def store_v(b, kt):
            n = keys_in(kt)
            sp.wait_ge(v_ev, 2 * (KT * b + kt + 1))
            sp.dma_start(VB[bass.ds(b, 1), 0:n, kt, :, :].rearrange("a p g d -> p (a g) d"),
                         v_stage[kt % 2][0:n, :].rearrange("p (g d) -> p g d", d=HD))\
              .then_inc(v_st[kt % 2], 16)

        def kv_round(b, first, last):
            if not first:
                for kt in range(KT):
                    store_v(b - 1, kt)
            if not last:
                sp.wait_ge(c_t, KT * (b + 1))
                load_ctx(b + 1)
            for h in range(KVH):
                sp.wait_ge(k_ev, 4 * (KVH * b + h + 1))
                sp.dma_start(k_dram[bass.ds(b * KVH + h, 1), :, :].rearrange("a p n -> (a p) n"),
                             k_stage[h % 2][:, :]).then_inc(k_st[h % 2], 16)

        kv_round(0, True, False)
        with sp.Fori(1, BATCH - 1) as b:
            kv_round(b, False, False)
        kv_round(BATCH - 1, False, True)
        for kt in range(2):
            store_v(BATCH - 1, kt)
        for i in range(2):
            sp.wait_ge(q_st[i], 16 * HEADS // 2)
            sp.wait_ge(k_st[i], 16 * BATCH * KVH // 2)

        def load_k(i, g, b):
            need(sp, k_split, i)
            sp.dma_start(k_raw[:, :], k_dram[bass.ds(b * KVH + g, 1), :, :].rearrange("a p n -> (a p) n"))\
              .then_inc(k_ld, 16)

        def load_v(i, g, b):
            need(sp, v_split, i)
            src = v_dram[bass.ds(b * KVH + g, 1), :, :].rearrange("a p n -> (a p) n")
            sp.dma_start(v_raw[:, 0:KT - 1, :], src[:, 0:(KT - 1) * HD].rearrange("p (t d) -> p t d", d=HD))\
              .then_inc(v_ld, 16)
            sp.dma_start(v_raw[0:TAIL, KT - 1, :], src[0:TAIL, (KT - 1) * HD:KT * HD]).then_inc(vt_ld, 16)

        def load_q(n, g, b, j):
            need(sp, q_split, n - 1)
            sp.dma_start(q_raw[j][:, :, :],
                         Q_B[bass.ds(GQ * g + 2 * j, 2), :, b, :].rearrange("h d t -> d h t"))\
              .then_inc(q_ld[j], 16)

        def load_wo(g):
            need(sp, wo_split, 2 * g)
            sp.dma_start(wo_raw[:, :, :], Wo[bass.ds(g * GQ * HD, GQ * HD), :]
                         .rearrange("(h d) n -> d h n", d=HD)).then_inc(wo_ld, 16)

        def a_loads(g, first):
            for b in range(BATCH):
                i = BATCH * g + b
                load_k(i, g, b)
                load_q(2 * i, g, b, 0)
                if b == 1:
                    load_wo(g)
                load_q(2 * i + 1, g, b, 1)
                if first and b == 0:
                    for kt in range(2, KT):
                        store_v(BATCH - 1, kt)
                    sp.wait_ge(v_st[0], 16 * BATCH * ((KT + 1) // 2))
                    sp.wait_ge(v_st[1], 16 * BATCH * (KT // 2))
                load_v(i, g, b)
                if first and b == 0:
                    for t in range(NT):
                        sp.dma_start(acc[:, t, :], bo.partition_broadcast(P)).then_inc(acc_0, 16)

        a_loads(0, True)
        with sp.Fori(1, KVH) as g:
            a_loads(g, False)

        sp.wait_ge(t_mm, KT * (NSTEP - 1))
        sp.dma_start(gates[:, 0:1], g_xattn.partition_broadcast(P)).then_inc(fx_ld, 16)
        sp.dma_start(gates[:, 1:2], g_ffn.partition_broadcast(P)).then_inc(fx_ld, 16)
        sp.dma_start(xr[:, :, :], X_V).then_inc(fx_ld, 16)
        sp.dma_start(bb_bc[:, :], b_base.partition_broadcast(P)).then_inc(fx_ld, 16)
        for t in range(NT):
            sp.wait_ge(f_fin, t + 1)
            sp.dma_start(OUT_V[t], f_o[t % 2][:, :]).then_inc(f_st[t % 2], 16)
        for i in range(2):
            sp.wait_ge(f_st[i], 16 * NT // 2)

    @block.gpsimd
    def _(pool):
        pool.memset(ident[:, :], 0.0).then_inc(id_rdy, 1)
        pool.memset(half_neg[:, :], -0.5).then_inc(cst, 1)
        pool.wait_ge(id_rdy, 1)
        pool.affine_select(out=ident[:, :], in_=ident[:, :], compare_op=ALU.not_equal, fill=1.0,
                           base=0, pattern=[[-1, P]], channel_multiplier=1).then_inc(id_rdy, 1)
        pool.wait_ge(cst, 1)
        for i in range(NT // 2):
            pool.wait_ge(x_var, i + 1)
            two = slice(2 * i, 2 * i + 2)
            pool.tensor_tensor(rstd[:, two], veps[:, two], half_neg[:, two], ALU.pow).then_inc(x_rstd, 1)

        def split(raw, hi, lo, hi_s, n, split_s):
            pool.sem_inc(split_go, 1)
            pool.tensor_scalar(hi, raw, 1.0, 0.0, ALU.mult, ALU.add).then_inc(hi_s, 1)
            pool.wait_ge(hi_s, n + 1)
            pool.tensor_tensor(lo, raw, f32(hi), ALU.subtract).then_inc(split_s, 1)

        def q_round(g, first):
            for hh in range(GQ):
                h = GQ * g + hh
                pool.wait_ge(wq_ld[hh], 16 * (g + 1))
                if not first:
                    pool.wait_ge(q_mm, 2 * (h - GQ + 1))
                split(wq_raw[hh][:, :, :], wq[hh][0][:, :, :], wq[hh][1][:, :, :], wq_hi_s, h, wq_split)

        q_round(0, True)
        with pool.Fori(1, KVH) as g:
            q_round(g, False)

        pool.wait_ge(k_mm, 4 * BATCH * KVH)
        for i in range(2):
            for part in kh[i]:
                pool.memset(f32(part[:, KEYS:KEYS_E]), 0.0).then_inc(pad, 1)

        def a_splits(g, first):
            for b in range(BATCH):
                i = BATCH * g + b
                pool.wait_ge(k_ld, 16 * (i + 1))
                if not first or i >= 2:
                    pool.wait_ge(s_mm, 24 * (i - 1))
                split(k_raw[:, :], kh[b % 2][0][:, 0:KEYS], kh[b % 2][1][:, 0:KEYS], k_hi_s, i, k_split)
                for j in range(2):
                    n = 2 * i + j
                    if b == 1:
                        pool.wait_ge(wo_ld, 16 * (g + 1))
                        if not first:
                            pool.wait_ge(o_mm, 4 * (PG * g - 1 + j))
                        else:
                            pool.wait_ge(v_mm, 2 * KT * BATCH)
                        two = slice(2 * j, 2 * j + 2)
                        split(wo_raw[:, two, :], wo[0][:, two, :], wo[1][:, two, :], wo_hi_s,
                              2 * g + j, wo_split)
                    pool.wait_ge(q_ld[j], 16 * (i + 1))
                    if not first or n >= 2:
                        pool.wait_ge(s_mm, 12 * (n - 1))
                    split(q_raw[j][:, :, :].rearrange("p h t -> p (h t)"), qh[j][0][:, :],
                          qh[j][1][:, :], q_hi_s, n, q_split)
                pool.wait_ge(v_ld, 16 * (i + 1))
                pool.wait_ge(vt_ld, 16 * (i + 1))
                if first and b == 1:
                    pool.wait_ge(v_mm, 2 * KT * BATCH)
                if not first or i >= 2:
                    pool.wait_ge(pv_mm, KT * (2 * i - 2))
                hi, lo = vh[b % 2]
                full = slice(0, KT - 1)
                pool.sem_inc(split_go, 1)
                pool.tensor_scalar(hi[:, full, :], v_raw[:, full, :], 1.0, 0.0, ALU.mult, ALU.add)\
                    .then_inc(v_hi_s, 1)
                pool.tensor_scalar(hi[0:TAIL, KT - 1, :], v_raw[0:TAIL, KT - 1, :], 1.0, 0.0,
                                   ALU.mult, ALU.add).then_inc(v_hi_s, 1)
                pool.wait_ge(v_hi_s, 2 * i + 2)
                pool.tensor_tensor(lo[:, full, :], v_raw[:, full, :], f32(hi[:, full, :]), ALU.subtract)
                pool.tensor_tensor(lo[0:TAIL, KT - 1, :], v_raw[0:TAIL, KT - 1, :],
                                   f32(hi[0:TAIL, KT - 1, :]), ALU.subtract).then_inc(v_split, 1)

        a_splits(0, True)
        with pool.Fori(1, KVH) as g:
            a_splits(g, False)

        pool.wait_ge(t_mm, KT * (NSTEP - 1))
        pool.iota(iota_e[:, :], [[1, EXPERTS]], base=0, channel_multiplier=0,
                  allow_small_or_imprecise_dtypes=True).then_inc(g_rdy, 1)
        for t in range(NT):
            pool.wait_ge(f_var, t + 1)
            pool.tensor_tensor(rstd[:, t:t + 1], veps[:, t:t + 1], half_neg[:, t:t + 1], ALU.pow)\
                .then_inc(f_rstd, 1)
            pool.wait_ge(f_x1_s, t + 1)
            if t == 0:
                pool.wait_ge(f_bias, 1)
            need(pool, f_fin, t - 3)
            pool.tensor_tensor(f_x1b[t % 4][:, :], f_x1[t % 4][:, :], tgbb[:, :], ALU.add)\
                .then_inc(f_x1b_s, 1)

    @block.scalar
    def _(act):
        act.dma_start(bias_rows[0:HEADS, :], bq.rearrange("(h d) -> h d", d=HD)).then_inc(bias_ld, 16)
        act.dma_start(bias_rows[HEADS:HEADS + KVH, :], bkv[0:KVH * HD].rearrange("(h d) -> h d", d=HD))\
           .then_inc(bias_ld, 16)
        act.dma_start(ffn_raw[:, :, :], W_base.rearrange("(c p) n -> p c n", p=P)).then_inc(ffn_ld, 16)
        act.dma_start(A_raw[:, :], A_stack.rearrange("e r n -> (e r) n")).then_inc(ffn_ld, 16)
        act.dma_start(R_raw[:, :], W_router).then_inc(ffn_ld, 16)
        for c in range(DC):
            act.dma_start(B_raw[:, c, :].rearrange("p (e r) -> p e r", r=RANK),
                          B_stack[:, c * P:(c + 1) * P, :].rearrange("e p r -> p e r")).then_inc(ffn_ld, 16)

        act.dma_start(bv_bc[:, :], bkv[KVH * HD:2 * KVH * HD].partition_broadcast(P)).then_inc(bv_ld, 16)

        act.wait_ge(b_mm, 1)
        act.activation(bqT[:, :], bank(4, HEADS), ACT.Copy, scale=SCALE).then_inc(b_rdy, 1)
        act.activation(bkT[:, :], bank(4)[:, HEADS:HEADS + KVH], ACT.Copy).then_inc(b_rdy, 1)
        for t in range(NT):
            act.wait_ge(xT_mm, t + 1)
            act.activation(xT[0][:, :, t * P:(t + 1) * P],
                           bank(6 + t % 2).rearrange("p (k t) -> p k t", k=DC), ACT.Copy)\
               .then_inc(xT_hi_s, 1)
        act.dma_start(wkv_raw[0][:, :], WKV_V[0]).then_inc(wkv_ld, 16)
        for n in range(FFN_GROUPS):
            act.wait_ge(f_mm, n + 1)
            _, ro, co, dst = ffn_group(n)
            act.activation(dst, bank(4 + n % 2)[0:ro, :].rearrange("p (k n) -> p k n", k=DC)[:, :, 0:co],
                           ACT.Copy).then_inc(f_ev, 1)
        for k in range(DC):
            if k > 0:
                act.wait_ge(wkv_split, 2 * k)
                act.dma_start(wkv_raw[0][:, :], WKV_V[k]).then_inc(wkv_ld, 16)
            act.wait_ge(wkv_ld, 16 * (k + 1))
            act.activation(wk[0][:, k, :], wkv_raw[0][:, 0:KVH * HD], ACT.Copy).then_inc(wkv_hi_s, 1)
            act.activation(wv[0][:, k, :], wkv_raw[0][:, KVH * HD:], ACT.Copy).then_inc(wkv_hi_s, 1)
        def ctx_hi(b, kt):
            n = keys_in(kt)
            act.wait_ge(c_t, KT * b + kt + 1)
            act.activation(ctxT[0][:, :, kt * P:kt * P + n],
                           bank(ctx_bank(b, kt)).rearrange("p (k t) -> p k t", k=DC)[:, :, 0:n], ACT.Copy)\
               .then_inc(c_hi, 1)

        def kv_round(b, first):
            for kt in range(KT):
                ctx_hi(b, kt)
            for h in range(KVH):
                if not first or h >= 2:
                    act.wait_ge(k_st[h % 2], 16 * (4 * b + h // 2))
                for c, (at, _, valid) in enumerate(CHUNKS):
                    act.wait_ge(k_mm, 4 * (KVH * b + h) + c + 1)
                    act.activation(k_stage[h % 2][:, at:at + valid], bank(c, valid), ACT.Identity,
                                   bias=bkT[:, h:h + 1]).then_inc(k_ev, 1)

        kv_round(0, True)
        with act.Fori(1, BATCH) as b:
            kv_round(b, False)

        act.wait_ge(v_mm, 2 * KT * BATCH)

        def a_step(n, s, has_s, has_m):
            m = n - 1
            par = s % 2
            for kind, i in ACT_UNITS:
                if kind == "T" and has_m:
                    act.wait_ge(t_mm, KT * m + i + 1)
                    rows_n = keys_in(i)
                    need(act, pv_mm, KT * m + (i - 2 if i else 0))
                    act.activation(pT[i % 3][0][0:rows_n, :], bank(t_bank(i, s))[0:rows_n, :], ACT.Copy)\
                       .then_inc(pt_hi, 1)
                elif kind == "E" and has_s:
                    if i == 0 and (not isinstance(n, int) or n >= 2):
                        act.wait_ge(t_mm, KT * (n - 1))
                        act.wait_ge(rs_s, n - 1)
                    act.wait_ge(nm_s, 4 * n + i + 1)
                    act.activation(prob[par][i][:, 0:3 * CW].rearrange("p (c n) -> p c n", c=3),
                                   psum[:, 0:3 * BANK].rearrange("p (c n) -> p c n", c=3)[:, :, 0:CW],
                                   ACT.Exp, bias=nmax[:, i % 2, :], accum_out=rows[:, par, i, 0:1])\
                       .then_inc(ex_a, 1)
                elif kind == "F" and has_s:
                    act.activation(prob[par][i][:, 3 * CW:KEYS], bank(3, KEYS - 3 * CW), ACT.Exp,
                                   bias=nmax[:, i % 2, :], accum_out=rows[:, par, i, 1:2])\
                       .then_inc(ex_b, 1)
                elif kind == "N" and has_m:
                    if not has_s:
                        act.wait_ge(fx_ld, 64)
                        act.activation(tg[:, :], gates[:, :], ACT.Tanh).then_inc(g_rdy, 1)
                    act.wait_ge(pv_mm, KT * (m + 1))
                    need(act, o_mm, 4 * m)
                    act.activation(oT[0][:, :], bank(6), ACT.Copy).then_inc(o_hi_s, 1)

        for s in range(PG):
            a_step(s, s, True, s > 0)
        with act.Fori(1, KVH) as g:
            for s in range(PG):
                a_step(PG * g + s, s, True, True)
        a_step(NSTEP, 0, False, True)

        def xT_copy(t):
            p = t % 2
            act.wait_ge(f_tr, t + 1)
            act.activation(f_xT[p][:, :, :].rearrange("p k t -> p (k t)"), bank(5 + p), ACT.Copy)\
               .then_inc(f_xT_s, 1)

        xT_copy(0)
        xT_copy(1)
        for t in range(1, NT + 1):
            u = t - 1
            p = u % 2
            act.wait_ge(f_nm, u + 1)
            act.activation(f_sm[p][:, 8:16], bank(p, EXPERTS), ACT.Exp, bias=f_sm[p][:, 0:1],
                           accum_out=f_sm[p][:, 1:2]).then_inc(f_ex, 1)
            if t + 1 < NT:
                xT_copy(t + 1)
            act.wait_ge(f_ht, u + 1)
            act.activation(f_hT[p][:, :], bank(7, P), ACT.Copy).then_inc(f_hT_s, 1)

    @block.vector
    def _(dve):
        def x_stats(i):
            dve.wait_ge(x_ld[i], 16)
            for t in (2 * i, 2 * i + 1):
                dve.bn_stats(stats[:, t, :], xn[:, t, :]).then_inc(x_stat, 1)
            for t in (2 * i, 2 * i + 1):
                dve.wait_ge(x_stat, 2 * i + t + 1)
                dve.bn_aggr(mv[:, t, :], stats[:, t, :]).then_inc(x_stat, 1)
            dve.wait_ge(x_stat, 4 * i + 4)
            dve.tensor_scalar(veps[:, 2 * i:2 * i + 2], mv[:, 2 * i:2 * i + 2, 1], EPS, None, ALU.add)\
               .then_inc(x_var, 1)

        def xt_lo(t):
            dve.wait_ge(xT_hi_s, t + 1)
            sl = slice(t * P, (t + 1) * P)
            dve.tensor_tensor(xT[1][:, :, sl], bank(6 + t % 2).rearrange("p (k t) -> p k t", k=DC),
                              f32(xT[0][:, :, sl]), ALU.subtract).then_inc(xT_lo_s, 1)

        x_stats(0)
        x_stats(1)
        for i in range(NT // 2):
            dve.wait_ge(x_rstd, i + 1)
            for t in (2 * i, 2 * i + 1):
                dve.tensor_scalar(xn[:, t, :], xn[:, t, :], mv[:, t, 0:1], rstd[:, t:t + 1],
                                  ALU.subtract, ALU.mult).then_inc(xn_rdy, 1)
            if i + 2 < NT // 2:
                x_stats(i + 2)
            if i >= 1:
                xt_lo(2 * i - 2)
                xt_lo(2 * i - 1)
        xt_lo(NT - 2)
        xt_lo(NT - 1)

        def q_round(g, first):
            for hh in range(GQ):
                h = GQ * g + hh
                if not first or hh >= 2:
                    dve.wait_ge(q_st[hh % 2], 16 * (2 * g + hh // 2))
                for half in range(2):
                    dve.wait_ge(q_mm, 2 * h + half + 1)
                    dve.tensor_scalar(q_stage[hh % 2][:, half * BANK:(half + 1) * BANK],
                                      bank((hh % 2) * 2 + half), SCALE,
                                      bqT[:, bass.ds(GQ * g + hh, 1)], ALU.mult, ALU.add)\
                       .then_inc(q_ev, 1)

        dve.wait_ge(b_rdy, 2)
        q_round(0, True)
        for k in range(DC):
            q_round(k + 1, False)
            for i, (hi, lo) in enumerate((wk, wv)):
                dve.wait_ge(wkv_hi_s, 2 * k + i + 1)
                dve.tensor_tensor(lo[:, k, :], wkv_raw[0][:, i * KVH * HD:(i + 1) * KVH * HD],
                                  f32(hi[:, k, :]), ALU.subtract).then_inc(wkv_split, 1)
        with dve.Fori(DC + 1, KVH) as g:
            q_round(g, False)

        dve.wait_ge(q_mm, 2 * HEADS)
        dve.memset(f32(ctxT[0][:, :, KEYS:KEYS_E]), 0.0).then_inc(pad, 1)
        dve.memset(f32(ctxT[1][:, :, KEYS:KEYS_E]), 0.0).then_inc(pad, 1)
        dve.wait_ge(bv_ld, 16)

        def ctx_lo(b, kt):
            n = keys_in(kt)
            sl = slice(kt * P, kt * P + n)
            dve.wait_ge(c_hi, KT * b + kt + 1)
            dve.tensor_tensor(ctxT[1][:, :, sl],
                              bank(ctx_bank(b, kt)).rearrange("p (k t) -> p k t", k=DC)[:, :, 0:n],
                              f32(ctxT[0][:, :, sl]), ALU.subtract).then_inc(c_lo, 1)

        def v_evac(b, kt, first):
            n = keys_in(kt)
            if not first or kt >= 2:
                dve.wait_ge(v_st[kt % 2], 16 * ((KT + 1 - kt % 2) // 2 * b + kt // 2))
            for half in range(2):
                sl = slice(half * BANK, (half + 1) * BANK)
                dve.wait_ge(v_mm, 2 * (KT * b + kt) + half + 1)
                dve.tensor_tensor(v_stage[kt % 2][0:n, sl], bank(4 + half)[0:n, :], bv_bc[0:n, sl],
                                  ALU.add).then_inc(v_ev, 1)

        for kt in range(KT):
            ctx_lo(0, kt)
        for kt in range(KT):
            if kt == 0:
                dve.wait_ge(q_st[0], 16 * HEADS // 2)
            v_evac(0, kt, True)
            ctx_lo(1, kt)
        with dve.Fori(2, BATCH) as b:
            for kt in range(KT):
                v_evac(b - 1, kt, False)
                ctx_lo(b, kt)
        for kt in range(KT):
            v_evac(BATCH - 1, kt, False)

        count = [0]

        def step(ins):
            count[0] += 1
            ins.then_inc(fv, 1)
            dve.wait_ge(fv, count[0])

        def norm_stats(t):
            x1 = f_x1[t % 4]
            need(dve, f_x1b_s, t - 3)
            dve.scalar_tensor_tensor(x1[:, :], acc[:, t, :], tg[:, 0:1], xr[:, t, :],
                                     ALU.mult, ALU.add).then_inc(f_x1_s, 1)
            dve.wait_ge(f_x1_s, t + 1)
            step(dve.bn_stats(stats[:, t, :], x1[:, :]))
            step(dve.bn_aggr(mv[:, t, :], stats[:, t, :]))
            dve.tensor_scalar(veps[:, t:t + 1], mv[:, t, 1:2], EPS, None, ALU.add).then_inc(f_var, 1)

        def norm_apply(t):
            dve.wait_ge(f_rstd, t + 1)
            need(dve, f_tr, t - 1)
            dve.tensor_scalar(f_xn[t % 2][:, :], f_x1[t % 4][:, :], mv[:, t, 0:1], rstd[:, t:t + 1],
                              ALU.subtract, ALU.mult).then_inc(f_xn_s, 1)

        def router_max(t):
            dve.wait_ge(f_ra, t + 1)
            dve.tensor_reduce(f_sm[t % 2][:, 0:1], bank(t % 2, EXPERTS), AX.X, ALU.max, negate=True)\
               .then_inc(f_nm, 1)

        def router(t):
            p = t % 2
            sm = f_sm[p]
            dve.wait_ge(f_ex, t + 1)
            step(dve.reciprocal(sm[:, 2:3], sm[:, 1:2]))
            step(dve.tensor_scalar(sm[:, 16:24], sm[:, 8:16], sm[:, 2:3], None, ALU.mult))
            step(dve.max(sm[:, 24:32], sm[:, 16:24]))
            dve.max_index(f_ix[p][:, :], sm[:, 24:32], sm[:, 16:24]).then_inc(f_idx, 1)
            step(dve.tensor_tensor(sm[:, 3:4], sm[:, 24:25], sm[:, 25:26], ALU.add))
            dve.wait_ge(f_idx, t + 1)
            dve.tensor_copy(sm[:, 32:34], f_ix[p][:, 0:2]).then_inc(f_place, 1)
            step(dve.reciprocal(sm[:, 4:5], sm[:, 3:4]))
            step(dve.tensor_scalar(sm[:, 34:36], sm[:, 24:26], sm[:, 4:5], LORA_SCALE,
                                   ALU.mult, ALU.mult))
            dve.wait_ge(f_place, t + 1)
            dve.tensor_scalar(sm[:, 40:48], iota_e[:, :], sm[:, 32:33], sm[:, 34:35],
                              ALU.is_equal, ALU.mult).then_inc(f_top1, 1)
            step(dve.tensor_scalar(sm[:, 48:56], iota_e[:, :], sm[:, 33:34], sm[:, 35:36],
                                   ALU.is_equal, ALU.mult))
            dve.wait_ge(f_top1, t + 1)
            step(dve.tensor_tensor(sm[:, 56:64], sm[:, 40:48], sm[:, 48:56], ALU.add))
            need(dve, f_ht, t - 1)
            dve.tensor_tensor(f_hc[p][:, :].rearrange("p (e r) -> p e r", r=RANK),
                              bank(p, EXPERTS + P)[:, EXPERTS:].rearrange("p (e r) -> p e r", r=RANK),
                              sm[:, 56:64].unsqueeze(2).to_broadcast([P, EXPERTS, RANK]),
                              ALU.mult).then_inc(f_hc_s, 1)

        def finish(t):
            dve.wait_ge(f_out, t + 1)
            dve.wait_ge(f_x1b_s, t + 1)
            if t >= 2:
                dve.wait_ge(f_st[t % 2], 16 * (t // 2))
            dve.scalar_tensor_tensor(f_o[t % 2][:, :], bank(2 + t % 3), tg[:, 1:2], f_x1b[t % 4][:, :],
                                     ALU.mult, ALU.add).then_inc(f_fin, 1)

        def a_step(n, s, has_s, has_m, has_o):
            m = n - 1
            par = s % 2
            for kind, i in DVE_UNITS:
                if kind == "A" and has_o:
                    mo = n - 2
                    t = 2 * (((s - 2) % PG) // 2) + i % 2
                    dve.wait_ge(o_mm, 4 * mo + i + 1)
                    dve.wait_ge(ri_s, mo + 1)
                    need(dve, o_add, 4 * mo + i - 1)
                    dve.scalar_tensor_tensor(acc[:, t, :], bank(7), rinv[:, par, i:i + 1], acc[:, t, :],
                                             ALU.mult, ALU.add).then_inc(o_add, 1)
                elif kind == "I" and has_m:
                    dve.wait_ge(ex_b, 4 * (m + 1))
                    need(dve, ri_s, m)
                    dve.tensor_tensor(rsum[:, :], rows[:, 1 - par, :, 0], rows[:, 1 - par, :, 1],
                                      ALU.add).then_inc(rs_s, 1)
                    dve.wait_ge(rs_s, m + 1)
                    need(dve, o_add, 4 * (m - 1))
                    dve.reciprocal(rinv[:, 1 - par, :], rsum[:, :]).then_inc(ri_s, 1)
                elif kind == "T" and has_m:
                    rows_n = keys_in(i)
                    dve.wait_ge(pt_hi, KT * m + i + 1)
                    dve.tensor_tensor(pT[i % 3][1][0:rows_n, :], bank(t_bank(i, s))[0:rows_n, :],
                                      f32(pT[i % 3][0][0:rows_n, :]), ALU.subtract).then_inc(pt_lo, 1)
                elif kind == "L" and has_m:
                    if not has_s:
                        dve.wait_ge(fx_ld, 64)
                        dve.wait_ge(g_rdy, 2)
                        norm_stats(0)
                        dve.tensor_scalar(tgbb[:, :], bb_bc[:, :], tg[:, 1:2], None, ALU.mult)\
                           .then_inc(f_bias, 1)
                        norm_apply(0)
                        norm_stats(1)
                    dve.wait_ge(o_hi_s, m + 1)
                    dve.tensor_tensor(oT[1][:, :], bank(6), f32(oT[0][:, :]), ALU.subtract)\
                       .then_inc(o_split, 1)
                elif kind == "M" and has_s:
                    qt, part = i // 4, i % 4
                    q = 4 * n + qt
                    if part == 0:
                        need(dve, nm_s, q - 1)
                        dve.wait_ge(s_mm, 3 * q + 1)
                        dve.tensor_reduce(mx[:, qt % 2, 0:1],
                                          psum[:, 0:2 * BANK].rearrange("p (c n) -> p c n", c=2)[:, :, 0:CW],
                                          AX.XY, ALU.max).then_inc(mx_s, 1)
                    elif part < 3:
                        c = part + 1
                        dve.wait_ge(s_mm, 3 * q + c)
                        dve.tensor_reduce(mx[:, qt % 2, part:part + 1], bank(c, CHUNKS[c][2]), AX.X,
                                          ALU.max).then_inc(mx_s, 1)
                    else:
                        dve.wait_ge(mx_s, 3 * q + 3)
                        need(dve, ex_b, q - 1)
                        dve.tensor_reduce(nmax[:, qt % 2, :], mx[:, qt % 2, :], AX.X, ALU.max,
                                          negate=True).then_inc(nm_s, 1)

        for s in range(PG):
            if s == 2:
                dve.wait_ge(acc_0, 16 * NT)
            a_step(s, s, True, s > 0, s > 1)
        with dve.Fori(1, KVH) as g:
            for s in range(PG):
                a_step(PG * g + s, s, True, True, True)
        a_step(NSTEP, 0, False, True, True)

        norm_apply(1)
        router_max(0)
        router(0)
        a_step(NSTEP + 1, 1, False, False, True)
        dve.wait_ge(o_add, 4 * NSTEP)
        for t in range(1, NT + 2):
            if t + 1 < NT:
                norm_stats(t + 1)
            if 2 <= t <= NT:
                router_max(t - 1)
            if t + 1 < NT:
                norm_apply(t + 1)
            if 2 <= t <= NT:
                router(t - 1)
            if t >= 2:
                finish(t - 2)

    @block.tensor
    def _(pe):
        pe.wait_ge(id_rdy, 2)
        pe.wait_ge(bias_ld, 32)
        nb = HEADS + KVH
        nc.tensor.transpose(bank(4, nb), bias_rows[:, :], ident[0:nb, 0:nb]).then_inc(b_mm, 1)

        def x_transposes(t):
            pe.wait_ge(xn_rdy, t + 1)
            need(pe, xT_lo_s, t - 1)
            for k in range(DC):
                last = nc.tensor.transpose(bank(6 + t % 2)[:, k * P:(k + 1) * P],
                                           xn[:, t, k * P:(k + 1) * P], ident[:, :])
            last.then_inc(xT_mm, 1)

        def ffn_transposes(n):
            if n == 0:
                pe.wait_ge(ffn_ld, 16 * (3 + DC))
                pe.wait_ge(b_rdy, 2)
            need(pe, f_ev, n - 1)
            sources, ro, co, _ = ffn_group(n)
            for k, src in enumerate(sources):
                last = nc.tensor.transpose(bank(4 + n % 2)[0:ro, k * P:k * P + co], src,
                                           ident[0:co, 0:co])
            last.then_inc(f_mm, 1)

        def q_round(g, first):
            for hh in range(GQ):
                h = GQ * g + hh
                if not first or hh >= 1:
                    pe.wait_ge(wq_split, h + 1)
                for half in range(2):
                    if not first or hh >= 2:
                        pe.wait_ge(q_ev, 2 * h + half - 3)
                    if first and hh == 0:
                        for t in range(half * NT // 2, (half + 1) * NT // 2):
                            x_transposes(t)
                        pe.wait_ge(xT_lo_s, (half + 1) * NT // 2)
                        pe.wait_ge(wq_split, 1)
                    sl = slice(half * BANK, (half + 1) * BANK)
                    for k in range(DC):
                        last = product(bank((hh % 2) * 2 + half),
                                       [w[:, k, :] for w in wq[hh]], [a[:, k, sl] for a in xT],
                                       k == 0, k == DC - 1)
                    last.then_inc(q_mm, 1)
                if first:
                    for n in range(2 * hh, min(2 * hh + 2, FFN_GROUPS)):
                        ffn_transposes(n)

        q_round(0, True)
        with pe.Fori(1, KVH) as g:
            q_round(g, False)

        def ctx_t(b, kt, first):
            n = keys_in(kt)
            if kt == 0:
                pe.wait_ge(ctx_ld, 16 * (b + 1))
            if kt == KT - 1:
                pe.wait_ge(ctx_tail_ld, 16 * (b + 1))
            if first and kt >= 4:
                pe.wait_ge(c_lo, kt - 3)
            elif not first:
                pe.wait_ge(c_lo, KT * b + (kt - 1 if kt else 0))
            for k in range(DC):
                last = nc.tensor.transpose(bank(ctx_bank(b, kt))[:, k * P:k * P + n],
                                           ctx_raw[0:n, kt, k * P:(k + 1) * P], ident[0:n, 0:n])
            last.then_inc(c_t, 1)

        def v_tile(b, kt, first):
            n = keys_in(kt)
            for half in range(2):
                if not first or kt >= 1:
                    pe.wait_ge(v_ev, 2 * (KT * b + kt) + half - 1)
                cols = slice(half * BANK, (half + 1) * BANK)
                for k in range(DC):
                    last = product(bank(4 + half)[0:n, :],
                                   [a[:, k, kt * P:kt * P + n] for a in ctxT],
                                   [w[:, k, cols] for w in wv], k == 0, k == DC - 1)
                last.then_inc(v_mm, 1)

        def k_chunk(b, h, c, first):
            at, w_, _ = CHUNKS[c]
            if not first:
                pe.wait_ge(k_ev, 4 * (KVH * b + h) + c - 3)
            for k in range(DC):
                last = product(bank(c, w_), [w[:, k, h * HD:(h + 1) * HD] for w in wk],
                               [a[:, k, at:at + w_] for a in ctxT], k == 0, k == DC - 1)
            last.then_inc(k_mm, 1)

        def k_heads(b):
            pe.wait_ge(c_lo, KT * (b + 1))
            for h in range(KVH):
                for c in range(len(CHUNKS)):
                    k_chunk(b, h, c, False)

        done = 0
        for c, (at, w_, valid) in enumerate(CHUNKS):
            tiles = -(-(at + valid) // P)
            ahead = min(KT, tiles + (CW + P - 1) // P - 1)
            for kt in range(done, ahead):
                ctx_t(0, kt, True)
            done = ahead
            if c == 0:
                pe.wait_ge(wkv_split, 2 * DC)
                pe.wait_ge(pad, 2)
                pe.wait_ge(q_ev, 2 * HEADS)
            pe.wait_ge(c_lo, tiles)
            k_chunk(0, 0, c, True)
        for h in range(1, KVH):
            for c in range(len(CHUNKS)):
                k_chunk(0, h, c, False)
        for kt in range(KT):
            v_tile(0, kt, True)
            ctx_t(1, kt, False)
        k_heads(1)
        with pe.Fori(2, BATCH) as b:
            for kt in range(KT):
                v_tile(b - 1, kt, False)
                ctx_t(b, kt, False)
            k_heads(b)
        for kt in range(KT):
            v_tile(BATCH - 1, kt, False)

        def project(g, n, s, qt):
            mo = n - 2
            if qt == 0:
                pe.wait_ge(o_split, mo + 1)
                pe.wait_ge(wo_split, 2 * (g if s >= 2 else g - 1) + s % 2 + 1)
            need(pe, o_add, 4 * mo + qt)
            product(bank(7), [o[:, qt * P:(qt + 1) * P] for o in oT],
                    [w[:, 2 * (s % 2) + qt // 2, :] for w in wo], True, True).then_inc(o_mm, 1)

        def a_step(g, n, s, has_s, has_m, has_o):
            m = n - 1
            i_m = ((s - 1) % PG) // 2
            for unit in PE_UNITS:
                if unit[0] == "O" and has_o:
                    project(g, n, s, unit[1])
                elif unit[0] == "T" and has_m:
                    kt = unit[1]
                    if kt == 0:
                        pe.wait_ge(ex_b, 4 * (m + 1))
                    need(pe, pt_lo, KT * m + kt - 1)
                    n_out = keys_in(kt)
                    for qt in range(4):
                        last = nc.tensor.transpose(bank(t_bank(kt, s))[0:n_out, qt * P:(qt + 1) * P],
                                                   prob[1 - s % 2][qt][:, kt * P:kt * P + n_out],
                                                   ident[:, :])
                    last.then_inc(t_mm, 1)
                elif unit[0] == "P" and has_m:
                    kt = unit[1]
                    n_k = keys_in(kt)
                    pe.wait_ge(pt_lo, KT * m + kt + 1)
                    if kt == 0:
                        need(pe, o_split, m)
                        pe.wait_ge(v_split, BATCH * (g if s >= 1 else g - 1) + i_m + 1)
                    product(bank(6), [v[0:n_k, kt, :] for v in vh[i_m % 2]],
                            [t[0:n_k, :] for t in pT[kt % 3]], kt == 0, kt == KT - 1)\
                        .then_inc(pv_mm, 1)
                elif unit[0] == "S" and has_s:
                    qt, c = unit[1:]
                    q = 4 * n + qt
                    b = s // 2
                    if qt == 0 and c == 0:
                        pe.wait_ge(k_split, BATCH * g + b + 1)
                        pe.wait_ge(q_split, n + 1)
                    if c == 0:
                        need(pe, ex_a, q)
                    if c == 3:
                        need(pe, ex_b, q)
                    at, w_, _ = CHUNKS[c]
                    hh, tt = qt // 2, qt % 2
                    col = hh * TOK + tt * P
                    last = product(bank(c, w_), [a[:, col:col + P] for a in qh[s % 2]],
                                   [a[:, at:at + w_] for a in kh[b % 2]], True, True)
                    if c >= 1:
                        last.then_inc(s_mm, 1)

        pe.wait_ge(pad, 6)
        pe.wait_ge(v_ev, 2 * KT * BATCH)
        for s in range(PG):
            a_step(0, s, s, True, s > 0, s > 1)
        with pe.Fori(1, KVH) as g:
            for s in range(PG):
                a_step(g, PG * g + s, s, True, True, True)
        a_step(KVH, NSTEP, 0, False, True, True)

        def xn_transposes(t):
            p = t % 2
            pe.wait_ge(f_xn_s, t + 1)
            need(pe, f_xT_s, t - 1)
            for k in range(DC):
                last = nc.tensor.transpose(bank(5 + p)[:, k * P:(k + 1) * P],
                                           f_xn[p][:, k * P:(k + 1) * P], ident[:, :])
            last.then_inc(f_tr, 1)

        def router_and_a(t):
            p = t % 2
            pe.wait_ge(f_xT_s, t + 1)
            need(pe, f_hc_s, t - 1)
            for k in range(DC):
                last = nc.tensor.matmul(bank(p, EXPERTS + P), f_xT[p][:, k, :], RAT[:, k, :],
                                        start=k == 0, stop=k == DC - 1)
            last.then_inc(f_ra, 1)

        def base_layer(t, k):
            if k == 0 and t >= 3:
                pe.wait_ge(f_fin, t - 2)
            nc.tensor.matmul(bank(2 + t % 3), f_xT[t % 2][:, k, :], WbT[:, k, :],
                             start=k == 0, stop=False)

        def hidden_transpose(t):
            pe.wait_ge(f_hc_s, t + 1)
            need(pe, f_hT_s, t)
            nc.tensor.transpose(bank(7, P), f_hc[t % 2][:, :], ident[:, :]).then_inc(f_ht, 1)

        def experts_out(t):
            pe.wait_ge(f_hT_s, t + 1)
            nc.tensor.matmul(bank(2 + t % 3), f_hT[t % 2][:, :], BT[:, :], start=False, stop=True)\
                .then_inc(f_out, 1)

        xn_transposes(0)
        router_and_a(0)
        xn_transposes(1)
        for k in range(DC):
            base_layer(0, k)
            project(KVH, NSTEP + 1, 1, k)
        pe.wait_ge(o_add, 4 * NSTEP)
        for t in range(1, NT + 1):
            if t < NT:
                router_and_a(t)
            if t + 1 < NT:
                xn_transposes(t + 1)
            if t < NT:
                base_layer(t, 0)
                base_layer(t, 1)
            hidden_transpose(t - 1)
            if t < NT:
                base_layer(t, 2)
                base_layer(t, 3)
            experts_out(t - 1)

    es.close()


_INS = ["x", "ctx_4096", "g_xattn", "g_ffn", "L0_xattn_Wq", "L0_xattn_bq", "L0_xattn_Wkv",
        "L0_xattn_bkv", "L0_xattn_Wo", "L0_xattn_bo", "L0_ffn_W_base", "L0_ffn_b_base",
        "L0_ffn_W_router", "L0_ffn_A_stack", "L0_ffn_B_stack"]
_OUT = ((4, 256, 512), "float32")


def kernel(**inputs):
    import numpy as _np
    import concourse.bacc as _bacc
    from concourse import mybir as _mybir
    from concourse.bass_utils import run_bass_kernel_spmd as _run

    nc = _bacc.Bacc("TRN2", target_bir_lowering=False, num_devices=1)
    arrays, args = {}, []
    for name in _INS:
        a = _np.ascontiguousarray(inputs[name])
        arrays[f"in_{name}"] = a
        args.append(nc.dram_tensor(f"in_{name}", a.shape, _mybir.dt.from_np(a.dtype), kind="ExternalInput").ap())
    shape, dtype = _OUT
    args.append(nc.dram_tensor("out", shape, _mybir.dt.from_np(_np.dtype(dtype)), kind="ExternalOutput").ap())
    build(nc, *args)
    r = _run(nc, [arrays], core_ids=[0])
    return r.results[0]["out"]
```
